# Optimizing a Trainium2 kernel written in Bass

```python
import numpy as np
import jax
import jax.numpy as jnp

def _softmax(x, axis=-1):
    return jax.nn.softmax(x, axis=axis)

def _gelu(x):
    return jax.nn.gelu(x, approximate=True)

def _silu(x):
    return jax.nn.silu(x)

def _sigmoid(x):
    return jax.nn.sigmoid(x)

def _layernorm(x, axis=-1, eps=1e-05):
    m = jnp.mean(x, axis=axis, keepdims=True)
    v = jnp.var(x, axis=axis, keepdims=True)
    return (x - m) / jnp.sqrt(v + eps)

def _scatter_add(tgt, idx, src, axis=0):
    return tgt.at[idx].add(src)

def _segment_sum(src, seg, n):
    return jax.ops.segment_sum(src, seg, n)
kernel_name = 'mk_gnn_preln_d4_gnn_r32_dc3f7c'

def setup_inputs(seed: int=0):
    np.random.seed(seed)
    _w = jnp.asarray

    def _rec_inputs():
        import jax
        import jax.numpy as jnp
        _gk = jax.random.key(seed)
        x = -0.0001006 + 1 * jax.random.normal(jax.random.fold_in(_gk, 1), (50000, 96), jnp.float32)
        src = jax.random.randint(jax.random.fold_in(_gk, 2), (50000,), 0, 50000, jnp.int32)
        dst = jax.random.randint(jax.random.fold_in(_gk, 3), (50000,), 0, 50000, jnp.int32)
        _o = jnp.argsort(dst, stable=True)
        src = src[_o]
        dst = dst[_o]
        edge_attr_32 = 0.000196303 + 1.00016 * jax.random.normal(jax.random.fold_in(_gk, 11), (50000, 32), jnp.float32)
        edge_attr_96 = 5.93493e-05 + 1.00006 * jax.random.normal(jax.random.fold_in(_gk, 12), (50000, 96), jnp.float32)
        edge_weight = jax.random.uniform(jax.random.fold_in(_gk, 14), (50000,), jnp.float32, 0.0, 1)
        return (x, src, dst, edge_attr_32, edge_attr_96, edge_weight)
    x, src, dst, edge_attr_32, edge_attr_96, edge_weight = _rec_inputs()

    def _L0_gnn_setup():
        import jax, jax.numpy as jnp
        import numpy as np
        N_NODES = 50000
        N_EDGES = 25000
        IN_DIM = 96
        NUM_HEADS = 8
        HEAD_DIM = IN_DIM // NUM_HEADS
        key = jax.random.key(seed)
        ks = jax.random.split(key, 11)
        s = 1.0 / np.sqrt(IN_DIM)
        return {'x': jax.random.normal(ks[0], (N_NODES, IN_DIM), dtype=jnp.float32), 'edge_index': jax.random.randint(ks[1], (2, N_EDGES), 0, N_NODES, dtype=jnp.int64), 'edge_attr': jax.random.normal(ks[2], (N_EDGES, IN_DIM), dtype=jnp.float32), 'Wq': jax.random.normal(ks[3], (IN_DIM, IN_DIM), dtype=jnp.float32) * s, 'bq': jax.random.normal(ks[4], (IN_DIM,), dtype=jnp.float32) * s, 'Wk': jax.random.normal(ks[5], (IN_DIM, IN_DIM), dtype=jnp.float32) * s, 'bk': jax.random.normal(ks[6], (IN_DIM,), dtype=jnp.float32) * s, 'We': jax.random.normal(ks[7], (IN_DIM, IN_DIM), dtype=jnp.float32) * s, 'be': jax.random.normal(ks[8], (IN_DIM,), dtype=jnp.float32) * s, 'Wv': jax.random.normal(ks[9], (IN_DIM, IN_DIM), dtype=jnp.float32) * s, 'bv': jax.random.normal(ks[10], (IN_DIM,), dtype=jnp.float32) * s}
    _L0_gnn_all = _L0_gnn_setup()
    _L0_gnn_in = {k: v for k, v in _L0_gnn_all.items() if k in ('Wq', 'bq', 'Wk', 'bk', 'We', 'be', 'Wv', 'bv')}
    del _L0_gnn_all

    def _L1_gnn_setup():
        import jax, jax.numpy as jnp
        import numpy as np
        N, E = (50000, 25000)
        ND, ED = (96, 32)

        def _gelu(x):
            return jax.nn.gelu(x, approximate=False)
        key = jax.random.key(seed)
        ks = jax.random.split(key, 16)
        s = lambda fan_in: 1.0 / np.sqrt(fan_in)
        inp = {'x': jax.random.normal(ks[0], (N, ND), jnp.float32), 'edge_index': jax.random.randint(ks[1], (2, E), 0, N, jnp.int32), 'edge_attr': jax.random.normal(ks[2], (E, ED), jnp.float32), 'mW1': jax.random.uniform(ks[3], (ND + ED, ND), jnp.float32, -s(ND + ED), s(ND + ED)), 'mb1': jnp.zeros((ND,), jnp.float32), 'mW2': jax.random.uniform(ks[4], (ND, ND), jnp.float32, -s(ND), s(ND)), 'mb2': jnp.zeros((ND,), jnp.float32), 'gW1': jax.random.uniform(ks[5], (ND + ED, ND), jnp.float32, -s(ND + ED), s(ND + ED)), 'gb1': jnp.zeros((ND,), jnp.float32), 'gW2': jax.random.uniform(ks[6], (ND, 1), jnp.float32, -s(ND), s(ND)), 'gb2': jnp.zeros((1,), jnp.float32), 'uW1': jax.random.uniform(ks[7], (2 * ND, ND), jnp.float32, -s(2 * ND), s(2 * ND)), 'ub1': jnp.zeros((ND,), jnp.float32), 'uW2': jax.random.uniform(ks[8], (ND, ND), jnp.float32, -s(ND), s(ND)), 'ub2': jnp.zeros((ND,), jnp.float32), 'ln_g': jnp.ones((ND,), jnp.float32), 'ln_b': jnp.zeros((ND,), jnp.float32)}
        return inp
    _L1_gnn_all = _L1_gnn_setup()
    _L1_gnn_in = {k: v for k, v in _L1_gnn_all.items() if k in ('mW1', 'mb1', 'mW2', 'mb2', 'gW1', 'gb1', 'gW2', 'gb2', 'uW1', 'ub1', 'uW2', 'ub2', 'ln_g', 'ln_b')}
    del _L1_gnn_all

    def _L2_gnn_setup():
        import jax, jax.numpy as jnp
        import numpy as np
        K = 16
        ALPHA = 0.1
        key = jax.random.key(seed)
        k1, k2 = jax.random.split(key)
        N, E, D = (50000, 25000, 96)
        x = jax.random.normal(k1, (N, D), dtype=jnp.float32)
        edge_index = jax.random.randint(k2, (2, E), 0, N, dtype=jnp.int64)
        return {'x': x, 'edge_index': edge_index}
    _L2_gnn_all = _L2_gnn_setup()
    _L2_gnn_in = {k: v for k, v in _L2_gnn_all.items() if k in ()}
    del _L2_gnn_all

    def _L3_gnn_setup():
        import jax, jax.numpy as jnp
        import numpy as np
        N_NODES = 50000
        N_EDGES = 25000
        D_IN = 96
        D_OUT = 96
        key = jax.random.key(seed)
        k1, k2, k3 = jax.random.split(key, 3)
        x = jax.random.normal(k1, (N_NODES, D_IN), dtype=jnp.float32)
        edge_index = jax.random.randint(k2, (2, N_EDGES), 0, N_NODES, dtype=jnp.int64)
        edge_weight = jnp.ones((N_EDGES,), dtype=jnp.float32)
        W = jax.random.normal(k3, (D_IN, D_OUT), dtype=jnp.float32) * (1.0 / np.sqrt(D_IN))
        b = jnp.zeros((D_OUT,), dtype=jnp.float32)
        return {'x': x, 'edge_index': edge_index, 'edge_weight': edge_weight, 'W': W, 'b': b}
    _L3_gnn_all = _L3_gnn_setup()
    _L3_gnn_in = {k: v for k, v in _L3_gnn_all.items() if k in ('W', 'b')}
    del _L3_gnn_all
    return {'x': x, 'src': src, 'dst': dst, 'edge_attr_32': edge_attr_32, 'edge_attr_96': edge_attr_96, 'edge_weight': edge_weight, 'L0_gnn_Wq': _L0_gnn_in['Wq'], 'L0_gnn_bq': _L0_gnn_in['bq'], 'L0_gnn_Wk': _L0_gnn_in['Wk'], 'L0_gnn_bk': _L0_gnn_in['bk'], 'L0_gnn_We': _L0_gnn_in['We'], 'L0_gnn_be': _L0_gnn_in['be'], 'L0_gnn_Wv': _L0_gnn_in['Wv'], 'L0_gnn_bv': _L0_gnn_in['bv'], 'L1_gnn_mW1': _L1_gnn_in['mW1'], 'L1_gnn_mb1': _L1_gnn_in['mb1'], 'L1_gnn_mW2': _L1_gnn_in['mW2'], 'L1_gnn_mb2': _L1_gnn_in['mb2'], 'L1_gnn_gW1': _L1_gnn_in['gW1'], 'L1_gnn_gb1': _L1_gnn_in['gb1'], 'L1_gnn_gW2': _L1_gnn_in['gW2'], 'L1_gnn_gb2': _L1_gnn_in['gb2'], 'L1_gnn_uW1': _L1_gnn_in['uW1'], 'L1_gnn_ub1': _L1_gnn_in['ub1'], 'L1_gnn_uW2': _L1_gnn_in['uW2'], 'L1_gnn_ub2': _L1_gnn_in['ub2'], 'L1_gnn_ln_g': _L1_gnn_in['ln_g'], 'L1_gnn_ln_b': _L1_gnn_in['ln_b'], 'L3_gnn_W': _L3_gnn_in['W'], 'L3_gnn_b': _L3_gnn_in['b']}

def reference(x, src, dst, edge_attr_32, edge_attr_96, edge_weight, L0_gnn_Wq, L0_gnn_bq, L0_gnn_Wk, L0_gnn_bk, L0_gnn_We, L0_gnn_be, L0_gnn_Wv, L0_gnn_bv, L1_gnn_mW1, L1_gnn_mb1, L1_gnn_mW2, L1_gnn_mb2, L1_gnn_gW1, L1_gnn_gb1, L1_gnn_gW2, L1_gnn_gb2, L1_gnn_uW1, L1_gnn_ub1, L1_gnn_uW2, L1_gnn_ub2, L1_gnn_ln_g, L1_gnn_ln_b, L3_gnn_W, L3_gnn_b):
    import jax
    import jax.numpy as jnp

    def _L0_gnn_ref(x, edge_index, edge_attr, Wq, bq, Wk, bk, We, be, Wv, bv):
        import jax, jax.numpy as jnp
        import numpy as np
        N_NODES = 50000
        N_EDGES = 25000
        IN_DIM = 96
        NUM_HEADS = 8
        HEAD_DIM = IN_DIM // NUM_HEADS
        N = x.shape[0]
        H, D = (NUM_HEADS, HEAD_DIM)
        Q_h = (x @ Wq + bq).reshape(N, H, D)
        K_h = (x @ Wk + bk).reshape(N, H, D)
        V_h = (x @ Wv + bv).reshape(N, H, D)
        E = (edge_attr @ We + be).reshape(-1, H, D)
        src_idx = edge_index[0]
        dst_idx = edge_index[1]
        src = K_h[src_idx]
        dest = Q_h[dst_idx]
        score = src * dest / jnp.sqrt(jnp.asarray(D, x.dtype))
        score = score * E
        score = jnp.exp(jnp.clip(score.sum(-1, keepdims=True), -5.0, 5.0))
        msg = V_h[src_idx] * score
        wV = jax.ops.segment_sum(msg, dst_idx, num_segments=N)
        Z = jax.ops.segment_sum(score, dst_idx, num_segments=N)
        h_out = wV / (Z + 1e-06)
        return h_out.reshape(N, H * D)

    def _L1_gnn_ref(x, edge_index, edge_attr, mW1, mb1, mW2, mb2, gW1, gb1, gW2, gb2, uW1, ub1, uW2, ub2, ln_g, ln_b):
        import jax, jax.numpy as jnp
        import numpy as np
        N, E = (50000, 25000)
        ND, ED = (96, 32)

        def _gelu(x):
            return jax.nn.gelu(x, approximate=False)
        src, dst = (edge_index[0], edge_index[1])
        edge_input = jnp.concatenate([x[src], edge_attr], axis=-1)
        messages = _gelu(edge_input @ mW1 + mb1) @ mW2 + mb2
        gates = jax.nn.sigmoid(_gelu(edge_input @ gW1 + gb1) @ gW2 + gb2)
        aggregated = jax.ops.segment_sum(messages * gates, dst, num_segments=x.shape[0])
        combined = jnp.concatenate([x, aggregated], axis=-1)
        update = _gelu(combined @ uW1 + ub1) @ uW2 + ub2
        h = x + update
        mu = jnp.mean(h, axis=-1, keepdims=True)
        var = jnp.mean(jnp.square(h - mu), axis=-1, keepdims=True)
        return (h - mu) * jax.lax.rsqrt(var + 1e-05) * ln_g + ln_b

    def _L2_gnn_ref(x, edge_index):
        import jax, jax.numpy as jnp
        import numpy as np
        K = 16
        ALPHA = 0.1
        N = x.shape[0]
        loop = jnp.arange(N, dtype=edge_index.dtype)
        row = jnp.concatenate([edge_index[0], loop])
        col = jnp.concatenate([edge_index[1], loop])
        deg = jax.ops.segment_sum(jnp.ones_like(col, dtype=x.dtype), col, num_segments=N)
        deg_inv_sqrt = jnp.where(deg > 0, jax.lax.rsqrt(jnp.maximum(deg, 1e-30)), 0.0)
        norm = (deg_inv_sqrt[row] * deg_inv_sqrt[col])[:, None]
        h = x
        for _ in range(K):
            h_neighbors = jax.ops.segment_sum(norm * h[row], col, num_segments=N)
            h = (1.0 - ALPHA) * h_neighbors + ALPHA * x
        return h

    def _L3_gnn_ref(x, edge_index, edge_weight, W, b):
        import jax, jax.numpy as jnp
        import numpy as np
        N_NODES = 50000
        N_EDGES = 25000
        D_IN = 96
        D_OUT = 96
        'PyG GCNConv: out = D^{-1/2} (A + I) D^{-1/2} (x @ W) + b.'
        N = x.shape[0]
        row, col = (edge_index[0], edge_index[1])
        loop = jnp.arange(N, dtype=edge_index.dtype)
        row = jnp.concatenate([row, loop])
        col = jnp.concatenate([col, loop])
        ew = jnp.concatenate([edge_weight, jnp.ones((N,), dtype=edge_weight.dtype)])
        deg = jax.ops.segment_sum(ew, col, num_segments=N)
        dinv = jnp.where(deg > 0, jax.lax.rsqrt(deg), 0.0)
        norm = dinv[row] * ew * dinv[col]
        h = x @ W
        msg = h[row] * norm[:, None]
        out = jax.ops.segment_sum(msg, col, num_segments=N)
        return out + b
    edge_index = jnp.stack([src, dst])
    h = jnp.maximum(_layernorm(x, axis=-1), 0.0)
    x = x + _L0_gnn_ref(h, edge_index, edge_attr_96, L0_gnn_Wq, L0_gnn_bq, L0_gnn_Wk, L0_gnn_bk, L0_gnn_We, L0_gnn_be, L0_gnn_Wv, L0_gnn_bv)
    h = jnp.maximum(_layernorm(x, axis=-1), 0.0)
    x = x + _L1_gnn_ref(h, edge_index, edge_attr_32, L1_gnn_mW1, L1_gnn_mb1, L1_gnn_mW2, L1_gnn_mb2, L1_gnn_gW1, L1_gnn_gb1, L1_gnn_gW2, L1_gnn_gb2, L1_gnn_uW1, L1_gnn_ub1, L1_gnn_uW2, L1_gnn_ub2, L1_gnn_ln_g, L1_gnn_ln_b)
    h = jnp.maximum(_layernorm(x, axis=-1), 0.0)
    x = x + _L2_gnn_ref(h, edge_index)
    h = jnp.maximum(_layernorm(x, axis=-1), 0.0)
    x = x + _L3_gnn_ref(h, edge_index, edge_weight, L3_gnn_W, L3_gnn_b)
    return x

_drawn_inputs = setup_inputs


def setup_inputs(seed=0):
    import zlib

    import numpy as np

    out = dict(_drawn_inputs(seed))
    spreads = {'L1_gnn_mb1': (0.0, 2.0),
     'L1_gnn_mb2': (0.0, 2.0),
     'L1_gnn_gb1': (0.0, 0.8),
     'L1_gnn_ub1': (0.0, 0.282),
     'L1_gnn_ub2': (0.0, 0.1),
     'L1_gnn_ln_g': (1.0, 0.2),
     'L1_gnn_ln_b': (0.0, 0.1),
     'L3_gnn_b': (0.0, 0.1)}
    factors = {'edge_attr_32': 8.0,
     'L0_gnn_bq': 8.0,
     'L0_gnn_bk': 7.582,
     'L0_gnn_be': 8.0,
     'L1_gnn_mW1': 8.0,
     'L1_gnn_mW2': 6.981,
     'L1_gnn_gW1': 8.0,
     'L1_gnn_gW2': 8.0}
    for name, (base, spread) in spreads.items():
        noise = np.random.default_rng([zlib.crc32(name.encode()), seed]).standard_normal(out[name].shape)
        drawn = base * np.exp(spread * noise) if base else spread * noise
        out[name] = jnp.asarray(drawn.astype(out[name].dtype))
    for name, factor in factors.items():
        out[name] = (out[name] * factor).astype(out[name].dtype)
    return out
```

```python
from contextlib import ExitStack

import concourse.bass as bass
from concourse import mybir

P = 128
N = 50000
D = 96
HEADS = 8
HD = D // HEADS
ED = 32
CH = -(-N // (P * 8)) * 8
J = 8
NB = CH // J
PAIRS = NB // 2
ROWS = P * CH
FULL = P - 1
TAIL = N - FULL * CH
SPLIT = 112
AUX = ROWS
REG = ROWS + P
ZROW = REG
VALUES = ROWS
ROUNDS = 16
ALPHA = 0.1
NONE = 65535
WZ = D + HEADS
TR = D + 1
assert NB % 2 == 1 and 0 < TAIL < CH

F32 = mybir.dt.float32
I32 = mybir.dt.int32
ALU = mybir.AluOpType
ACT = mybir.ActivationFunctionType
AX = mybir.AxisListType.X
EPS = 1e-5


class Own:

    def __init__(self, eng, sem, per_step=0):
        self.eng, self.sem, self.per_step = eng, sem, per_step
        self.first, self.base, self.n = 0, 0, 0

    def loop(self):
        self.first, self.n = self.n, 0

    def step(self, index):
        self.base, self.n = index * self.per_step + self.first, 0

    def add(self, ins):
        ins.then_inc(self.sem, 1)
        self.n += 1

    def settle(self):
        self.eng.wait_ge(self.sem, self.base + self.n)

    def do(self, ins):
        self.add(ins)
        self.settle()

    def end(self):
        assert self.n == self.per_step, (self.n, self.per_step)


class Stream:

    def __init__(self, pair):
        self.pair, self.base = pair, [0, 0]

    def __getitem__(self, h):
        return self.pair[h]

    def wait(self, eng, h, count):
        eng.wait_ge(self.pair[h], count + self.base[h])

    def close(self, passes=1):
        self.base[0] += 16 * J * (PAIRS + 1) * passes
        self.base[1] += 16 * J * PAIRS * passes


def batches(eng, step):
    step(0, 0)
    step(0, 1)
    with eng.Fori(1, PAIRS) as i:
        step(i, 0)
        step(i, 1)
    step(PAIRS, 0)


def ahead(eng, early, late):
    early(0, 0)
    early(0, 1)
    late(0, 0)
    early(1, 0)
    late(0, 1)
    with eng.Fori(1, PAIRS) as i:
        early(i, 1)
        late(i, 0)
        early(i + 1, 0)
        late(i, 1)
    late(PAIRS, 0)


def program(nc, x, src, dst, edge_attr_32, edge_attr_96, edge_weight,
            Wq, bq, Wk, bk, We, be, Wv, bv,
            mW1, mb1, mW2, mb2, gW1, gb1, gW2, gb2, uW1, ub1, uW2, ub2, ln_g, ln_b, W3, b3, out):
    V, A, T, G = nc.vector, nc.scalar, nc.tensor, nc.gpsimd
    outer = ExitStack()

    def dram(name, rows, width):
        return nc.dram_tensor(name, [rows, width], F32, kind="Internal").ap()

    kv_t = dram("kv_t", ROWS, 2 * D)
    q_t = dram("q_t", ROWS, D)
    info_t = dram("info_t", ROWS, 4)
    agg0_t = dram("agg0_t", REG + 1, WZ)
    agg1_t = dram("agg1_t", REG + 1, D)
    agg3_t = dram("agg3_t", REG + 1, D)
    x1_t = dram("x1_t", ROWS, D)
    x2_t = dram("x2_t", ROWS, D)
    x3_t = dram("x3_t", ROWS, D)
    rec_t = dram("rec_t", ROWS, TR)
    y_t = [dram(f"y{k}_t", VALUES + REG, D) for k in range(2)]
    c_t = dram("c_t", ROWS, D)
    z_t = dram("z_t", ROWS, D)
    x_tail = dram("x_tail", CH, D)
    e96_tail = dram("e96_tail", CH, D)
    e32_tail = dram("e32_tail", CH, ED)
    out_tail = dram("out_tail", CH, D)

    with outer:
        def sb(name, shape, dt=F32, ctx=outer):
            return ctx.enter_context(nc.sbuf_tensor(name, shape, dt))

        def ps(name, shape, ctx):
            return ctx.enter_context(nc.psum_tensor(name, shape, F32))

        s_stream = [Stream([nc.alloc_semaphore(name=f"gathered{k}_{h}") for h in range(2)]) for k in range(3)]
        s_single = nc.alloc_semaphore(name="gathered_single")
        of_pass = []

        def sem(name):
            of_pass.append(nc.alloc_semaphore(name=name))
            return of_pass[-1]

        def retire():
            with nc.Block() as block:
                @block.sync
                def _(sp):
                    for s in of_pass:
                        sp.sem_clear(s)
            for s in of_pass:
                nc.release_semaphore(s)
            of_pass.clear()

        def sems(name):
            return [sem(f"{name}_{h}") for h in range(2)]

        def cols(t, n, h):
            return t[:, bass.ds((2 * n + h) * J, J)]

        def rows_of(table, first, n, h):
            return table[first:first + ROWS, :].rearrange("(p j) d -> p j d", p=P)[:, bass.ds((2 * n + h) * J, J), :]

        def load_padded(eng, tile, whole, tail, n, h, done):
            v = whole[0:FULL * CH, :].rearrange("(p j) d -> p j d", j=CH)
            c = bass.ds((2 * n + h) * J, J)
            eng.dma_start(tile[0:SPLIT], v[0:SPLIT, c, :]).then_inc(done, 16)
            eng.dma_start(tile[SPLIT:FULL], v[SPLIT:FULL, c, :]).then_inc(done, 16)
            eng.dma_start(tile[FULL:P], tail.rearrange("(a j) d -> a j d", a=1)[:, c, :]).then_inc(done, 16)

        def load_column(eng, tile, vec, first, done):
            v = vec[first:first + FULL * CH].rearrange("(p j) -> p j", j=CH)
            rest = vec[first + FULL * CH:N].rearrange("(a j) -> a j", a=1)
            eng.dma_start(tile[0:SPLIT], v[0:SPLIT]).then_inc(done, 16)
            eng.dma_start(tile[SPLIT:FULL], v[SPLIT:FULL]).then_inc(done, 16)
            eng.dma_start(tile[FULL:P, 0:N - first - FULL * CH], rest).then_inc(done, 16)

        ident = sb("ident", [P, P])
        B = sb("B", [P, P])
        src_i = sb("src_i", [P, CH], I32)
        dst_i = sb("dst_i", [P, CH], I32)
        scan = sb("scan", [P, CH, 3])
        k_e = sb("k_e", [P, CH])
        k_z = sb("k_z", [P, 1])
        ptr_n = sb("ptr_n", [P, CH])
        ptr_i = sb("ptr_i", [P, CH], I32)
        yptr_i = sb("yptr_i", [P, CH], I32)
        root = sb("root", [P, CH])
        iroot = sb("iroot", [P, CH])
        dinv = sb("dinv", [P, CH])
        ptr_e = sb("ptr_e", [P, CH])
        eps = sb("eps", [P, 1])
        zeros = sb("zeros", [P, WZ])
        scan_s = sb("scan_s", [P, 2, J, 3])
        idx_s = sb("idx_s", [P, 2, J], I32)
        F = sb("F", [P, WZ])
        Z = sb("Z", [P, WZ])
        s_turn_v, s_turn_p, s_turn_s = (nc.alloc_semaphore(name=f"{e}_turns") for e in ("vector", "pool", "sync"))
        s_w = sem("weights_loaded")
        weight_loads = []

        def weight(name, parts, width, rows=D + 1):
            t = sb(name, [rows, width])
            for r0, r1, c0, c1, a in parts:
                weight_loads.append((t[r0:r1, c0:c1], a))
            return t

        def row(v):
            return v.rearrange("(a n) -> a n", a=1)

        def col(v):
            return v.rearrange("(n a) -> n a", a=1)

        w_kvq = weight("w_kvq", [(0, D, 0, D, Wk), (0, D, D, 2 * D, Wv), (0, D, 2 * D, 3 * D, Wq),
                                 (D, D + 1, 0, D, row(bk)), (D, D + 1, D, 2 * D, row(bv)),
                                 (D, D + 1, 2 * D, 3 * D, row(bq))], 3 * D)
        w_e = weight("w_e", [(0, D, 0, D, We), (D, D + 1, 0, D, row(be))], D)
        w_m1 = weight("w_m1", [(0, ED, 0, D, mW1[D:D + ED, :]), (ED, P, 0, D, mW1[0:D, :])], D, P)
        w_g1 = weight("w_g1", [(0, ED, 0, D, gW1[D:D + ED, :]), (ED, P, 0, D, gW1[0:D, :])], D, P)
        w_m2 = weight("w_m2", [(0, D, 0, D, mW2), (D, D + 1, 0, D, row(mb2))], D)
        w_g2 = weight("w_g2", [(0, D, 0, 1, gW2), (D, D + 1, 0, 1, row(gb2))], 1)
        w_ua = weight("w_ua", [(0, D, 0, D, uW1[0:D, :])], D, D)
        w_ub = weight("w_ub", [(0, D, 0, D, uW1[D:2 * D, :])], D, D)
        w_u2 = weight("w_u2", [(0, D, 0, D, uW2), (D, D + 1, 0, D, row(ub2))], D)
        w_3 = weight("w_3", [(0, D, 0, D, W3)], D, D)
        c_m1 = weight("c_m1", [(0, D, 0, 1, col(mb1))], 1, D)
        c_g1 = weight("c_g1", [(0, D, 0, 1, col(gb1))], 1, D)
        c_u1 = weight("c_u1", [(0, D, 0, 1, col(ub1))], 1, D)
        r_rows = weight("r_rows", [(0, 1, 0, D, row(ln_g)), (0, 1, D, 2 * D, row(ln_b)),
                                   (0, 1, 2 * D, 3 * D, row(b3))], 3 * D, 1)
        r_all = sb("r_all", [P, 3, D])

        def ln_vector(dve, own, n, h, xin, st, mv, rn, s_mv, s_sd, s_rn, ready=None):
            for j in range(J):
                last = V.bn_stats(st[:, h, j, :], xin[:, j, :])
            own.do(last)
            dve.sem_inc(s_turn_v)
            for j in range(J):
                last = V.bn_aggr(mv[:, h, j, :], st[:, h, j, :])
            last.then_inc(s_mv[h], 1)
            dve.wait_ge(s_sd[h], n + 1)
            own.do(V.reciprocal(rn[:, h, 0, :], rn[:, h, 2, :]))
            V.scalar_tensor_tensor(out=rn[:, h, 1, :], in0=mv[:, h, :, 0], scalar=-1.0, in1=rn[:, h, 0, :],
                                   op0=ALU.mult, op1=ALU.mult).then_inc(s_rn[h], 1)

        def ln_scalar(act, n, h, xin, to, mv, rn, s_mv, s_sd, s_rn, func):
            act.wait_ge(s_mv[h], n + 1)
            A.activation(rn[:, h, 2, :], mv[:, h, :, 1], ACT.Sqrt, bias=eps[:]).then_inc(s_sd[h], 1)
            act.wait_ge(s_rn[h], n + 1)
            for j in range(J):
                last = A.activation(to[:, j, :], xin[:, j, :], func, scale=rn[:, h, 0, j:j + 1],
                                    bias=rn[:, h, 1, j:j + 1])
            return last

        def gather_slots(act, m, h, index, s_idx, s_free, per, n=None):
            s_free.wait(act, h, per * m)
            A.copy(idx_s[:, h, :], cols(index, m if n is None else n, h)).then_inc(s_idx[h], 1)

        def gathers(table, to, h, done):
            G.sem_inc(s_turn_p)
            for j in range(J):
                G.indirect_dma_start(out=to(j), out_offset=None, in_=table,
                                     in_offset=bass.IndirectOffsetOnAxis(ap=idx_s[:, h, j:j + 1], axis=0)
                                     ).then_inc(done, 16)

        def scan_step(dve, own, n, h, w, g, S, s_s=None, done=None):
            for j in range(J):
                before = S[:, 1 - h, J - 1, 0:w] if j == 0 else S[:, h, j - 1, 0:w]
                own.add(V.scalar_tensor_tensor(out=S[:, h, j, 0:w], in0=before, scalar=scan_s[:, h, j, 0:1],
                                               in1=g[:, j, 0:w], op0=ALU.mult, op1=ALU.add))
                last = V.scalar_tensor_tensor(out=F[:, 0:w], in0=g[:, j, 0:w], scalar=scan_s[:, h, j, 1:2],
                                              in1=F[:, 0:w], op0=ALU.mult, op1=ALU.add)
                if j < J - 1 or s_s is None:
                    own.add(last)
                else:
                    last.then_inc(s_s[h], 1)
                own.settle()
            if s_s is not None:
                dve.wait_ge(s_s[h], done)

        def pointers(own, ptr, no, start, t, to, base):
            own.do(V.scalar_tensor_tensor(out=t, in0=ptr[:], scalar=-1.0, in1=start[:], op0=ALU.mult, op1=ALU.add))
            own.do(V.tensor_scalar(t, t, -float(base), None, ALU.add))
            own.do(V.tensor_tensor(t, t, no[:], ALU.mult))
            own.do(V.scalar_tensor_tensor(out=t, in0=ptr[:], scalar=float(base), in1=t, op0=ALU.add, op1=ALU.add))
            own.add(V.tensor_copy(to[:], t))

        with ExitStack() as ph:
            nxt_i = sb("nxt_i", [P, CH], I32, ph)
            dst_f = sb("dst_f", [P, CH], F32, ph)
            nxt_f = sb("nxt_f", [P, CH], F32, ph)
            wts = sb("wts", [P, CH], F32, ph)
            m = sb("m", [P, CH], F32, ph)
            fm = sb("fm", [P, CH], F32, ph)
            ones = sb("ones", [P, CH], F32, ph)
            cnt = sb("cnt", [P, CH], F32, ph)
            wsum = sb("wsum", [P, CH], F32, ph)
            row_i = sb("row_i", [P, CH], I32, ph)
            row_f = sb("row_f", [P, CH], F32, ph)
            aux_i = sb("aux_i", [P, 1], I32, ph)
            aux_f = sb("aux_f", [P, 1], F32, ph)
            tmp = sb("tmp", [P, CH], F32, ph)
            diag = sb("diag", [P, P], F32, ph)
            tri = sb("tri", [P, P], F32, ph)
            ends = sb("ends", [P, 2], F32, ph)
            carry = sb("carry", [P, 2], F32, ph)
            cz = sb("cz", [P, 1], F32, ph)
            seg = sb("seg", [P, CH, 4], F32, ph)
            seg_i = sb("seg_i", [P, CH], I32, ph)
            none = sb("none", [P, CH, 4], F32, ph)
            p_first = ps("p_first", [P, P], ph)
            p_carry = ps("p_carry", [P, 2], ph)
            s_pad, s_in, s_tail, s_init = sem("padding_set"), sem("edges_loaded"), sem("tails_written"), sem("info_set")
            s_iota, s_zero, s_v, s_diag, s_pf = (sem("iotas"), sem("zeros_set"), sem("graph_vector"),
                                                 sem("diag_ready"), sem("first_broadcast"))
            s_b, s_pc, s_bc = sem("b_and_ends"), sem("carry_summed"), sem("rows_broadcast")
            s_none = sem("none_ready")

            with nc.Block() as block:
                @block.sync
                def _(sp):
                    sp.wait_ge(s_pad, 4)
                    load_column(sp, dst_i, dst, 0, s_in)
                    load_column(sp, nxt_i, dst, 1, s_in)
                    load_column(sp, src_i, src, 0, s_in)
                    load_column(sp, wts, edge_weight, 0, s_in)
                    for to, a in weight_loads:
                        sp.dma_start(to, a).then_inc(s_w, 16)
                    sp.wait_ge(s_zero, 1)
                    for tail, whole, w in ((x_tail, x, D), (e96_tail, edge_attr_96, D), (e32_tail, edge_attr_32, ED)):
                        sp.dma_start(tail[0:TAIL, :], whole[FULL * CH:N, :]).then_inc(s_tail, 16)
                        sp.dma_start(tail[TAIL:TAIL + 96, :], zeros[0:96, 0:w]).then_inc(s_tail, 16)
                        sp.dma_start(tail[TAIL + 96:CH, :], zeros[0:CH - TAIL - 96, 0:w]).then_inc(s_tail, 16)
                    for t in (agg0_t, agg1_t, agg3_t):
                        sp.dma_start(t[ZROW:ZROW + 1, :], zeros[0:1, 0:t.shape[1]]).then_inc(s_tail, 16)
                    sp.wait_ge(s_none, 2)
                    sp.dma_start(info_t.rearrange("(p j) d -> p j d", p=P), none[:]).then_inc(s_init, 16)
                    sp.wait_ge(s_tail, 16 * 12)
                    sp.wait_ge(s_init, 16)
                    sp.wait_ge(s_w, 16 * len(weight_loads))

                @block.gpsimd
                def _(pool):
                    G.memset(ident[:], 0.0).then_inc(s_iota, 1)
                    pool.wait_ge(s_iota, 1)
                    G.affine_select(out=ident[:], in_=ident[:], compare_op=ALU.not_equal, fill=1.0, base=0,
                                    pattern=[[-1, P]], channel_multiplier=1).then_inc(s_iota, 1)
                    G.memset(tri[:], 1.0).then_inc(s_iota, 1)
                    pool.wait_ge(s_iota, 3)
                    G.affine_select(out=tri[:], in_=tri[:], compare_op=ALU.is_gt, fill=0.0, base=0,
                                    pattern=[[1, P]], channel_multiplier=-1).then_inc(s_iota, 1)
                    G.iota(row_i[:], [[1, CH]], base=0, channel_multiplier=CH).then_inc(s_iota, 1)
                    G.iota(aux_i[:], [[1, 1]], base=AUX, channel_multiplier=1).then_inc(s_iota, 1)
                    pool.wait_ge(s_w, 16 * len(weight_loads))
                    G.partition_broadcast(r_all[:].rearrange("p a d -> p (a d)"), r_rows[:]).then_inc(s_bc, 1)

                @block.tensor
                def _(pe):
                    pe.wait_ge(s_diag, 1)
                    T.matmul(p_first[:], ones[:, 0:P], diag[:], start=True, stop=True).then_inc(s_pf, 1)
                    pe.wait_ge(s_b, 1)
                    T.matmul(p_carry[:], B[:], ends[:], start=True, stop=True).then_inc(s_pc, 1)

                @block.vector
                def _(dve):
                    own = Own(dve, s_v)
                    V.memset(dst_i[:], NONE).then_inc(s_pad, 1)
                    V.memset(nxt_i[:], NONE).then_inc(s_pad, 1)
                    V.memset(src_i[:], 0).then_inc(s_pad, 1)
                    V.memset(wts[:], 0.0).then_inc(s_pad, 1)
                    V.memset(zeros[:], 0.0).then_inc(s_zero, 1)
                    own.add(V.memset(ones[:], 1.0))
                    own.add(V.memset(eps[:], EPS))
                    own.do(V.memset(none[:], 0.0))
                    V.memset(none[:, :, 0:1], float(ZROW)).then_inc(s_none, 2)
                    own.add(V.memset(m[:, 0:1], 0.0))
                    own.add(V.memset(seg[:], 0.0))
                    dve.wait_ge(s_in, 16 * 12)
                    dve.wait_ge(s_iota, 6)
                    own.add(V.tensor_copy(dst_f[:], dst_i[:]))
                    own.add(V.tensor_copy(nxt_f[:], nxt_i[:]))
                    own.add(V.tensor_copy(row_f[:], row_i[:]))
                    own.do(V.tensor_copy(aux_f[:], aux_i[:]))
                    own.settle()
                    V.tensor_scalar(diag[:], ident[:], dst_f[:, 0:1], None, ALU.mult).then_inc(s_diag, 1)
                    own.add(V.tensor_tensor(m[:, 1:CH], dst_f[:, 1:CH], dst_f[:, 0:CH - 1], ALU.is_equal))
                    own.do(V.tensor_scalar(fm[:], dst_f[:], dst_f[:, 0:1], None, ALU.is_equal))
                    own.add(V.tensor_tensor_scan(cnt[:], m[:], ones[:], 0.0, ALU.mult, ALU.add))
                    own.do(V.tensor_tensor_scan(wsum[:], m[:], wts[:], 0.0, ALU.mult, ALU.add))
                    own.add(V.tensor_copy(ends[:, 0:1], cnt[:, CH - 1:CH]))
                    own.add(V.tensor_copy(ends[:, 1:2], wsum[:, CH - 1:CH]))
                    dve.wait_ge(s_pf, 1)
                    own.do(V.tensor_scalar(B[:], p_first[:], dst_f[:, CH - 1:CH], None, ALU.is_equal))
                    V.tensor_tensor(B[:], B[:], tri[:], ALU.mult).then_inc(s_b, 1)
                    dve.wait_ge(s_pc, 1)
                    own.do(V.tensor_copy(carry[:], p_carry[:]))
                    own.add(V.scalar_tensor_tensor(out=cnt[:], in0=fm[:], scalar=carry[:, 0:1], in1=cnt[:],
                                                   op0=ALU.mult, op1=ALU.add))
                    own.add(V.scalar_tensor_tensor(out=wsum[:], in0=fm[:], scalar=carry[:, 1:2], in1=wsum[:],
                                                   op0=ALU.mult, op1=ALU.add))
                    own.do(V.reduce_sum(cz[:], fm[:], AX))
                    own.do(V.tensor_tensor(cz[:], cz[:], carry[:, 0:1], ALU.add))
                    own.add(V.tensor_scalar(cz[:], cz[:], 1.0, None, ALU.add))
                    own.do(V.tensor_scalar(tmp[:], cnt[:], 1.0, None, ALU.add))
                    own.add(V.reciprocal(k_e[:], tmp[:]))
                    own.do(V.reciprocal(k_z[:], cz[:]))
                    own.add(V.tensor_scalar(k_e[:], k_e[:], 1.0 - ALPHA, None, ALU.mult))
                    own.add(V.tensor_scalar(k_z[:], k_z[:], 1.0 - ALPHA, None, ALU.mult))
                    own.do(V.tensor_scalar(tmp[:], row_f[:], -1.0, aux_f[:], ALU.mult, ALU.add))
                    own.do(V.tensor_tensor(tmp[:], tmp[:], fm[:], ALU.mult))
                    own.add(V.tensor_tensor(seg[:, :, 0], tmp[:], row_f[:], ALU.add))
                    own.add(V.tensor_copy(seg[:, :, 1], cnt[:]))
                    own.add(V.tensor_copy(seg[:, :, 2], wsum[:]))
                    own.do(V.tensor_tensor(nxt_f[:], dst_f[:], nxt_f[:], ALU.is_equal))
                    own.do(V.scalar_tensor_tensor(out=tmp[:], in0=nxt_f[:], scalar=float(2 * NONE), in1=dst_f[:],
                                                  op0=ALU.mult, op1=ALU.add))
                    own.add(V.tensor_copy(seg_i[:], tmp[:]))
                    own.add(V.tensor_copy(scan[:, :, 0], m[:]))
                    own.add(V.tensor_copy(scan[:, :, 1], fm[:]))
                    own.do(V.tensor_copy(scan[:, :, 2], wts[:]))
                    own.do(V.tensor_scalar(tmp[:], dst_f[:], float(N), None, ALU.is_lt))
                    own.do(V.tensor_tensor(tmp[:], tmp[:], dst_f[:], ALU.mult))
                    own.do(V.tensor_copy(dst_i[:], tmp[:]))

            with ExitStack() as p0:
                xs = sb("n0_x", [P, 2, J, D], F32, p0)
                hh = sb("n0_h", [P, 2, J, D], F32, p0)
                hT = sb("n0_hT", [D + 1, 2, 2, 4 * P], F32, p0)
                kvq = sb("n0_kvq", [P, 2, J, 3 * D], F32, p0)
                st = sb("n0_st", [P, 2, J, 6], F32, p0)
                mv = sb("n0_mv", [P, 2, J, 2], F32, p0)
                rn = sb("n0_rn", [P, 2, 3, J], F32, p0)
                seg_s = sb("seg_s", [P, 2, J, 4], F32, p0)
                tp = [ps(f"n0_tp{g}", [P, 4 * P], p0) for g in range(2)]
                ob = [ps(f"n0_ob{k}", [P, 3 * D], p0) for k in range(4)]
                s_x, s_mv, s_sd, s_rn, s_h = (sems("n0_x_in"), sems("n0_stats"), sems("n0_root"), sems("n0_scale"),
                                              sems("n0_h_ready"))
                s_tp = [sems(f"n0_tp{g}_full") for g in range(2)]
                s_tc = [sems(f"n0_tp{g}_copied") for g in range(2)]
                s_om = [sems(f"n0_ob{k}_full") for k in range(4)]
                s_oc = [sems(f"n0_ob{k}_copied") for k in range(4)]
                s_st, s_sl, s_sc, s_own, s_one = (sems("n0_stored"), sems("n0_slots"), s_stream[0],
                                                  sem("n0_vector"), sem("n0_ones"))

                with nc.Block() as block:
                    @block.sync
                    def _(sp):
                        def load(n, h):
                            sp.wait_ge(s_h[h], n)
                            load_padded(sp, xs[:, h], x, x_tail, n, h, s_x[h])

                        def store(n, h):
                            for k in range(4):
                                sp.wait_ge(s_oc[k][h], 2 * n + 2)
                            sp.dma_start(rows_of(kv_t, 0, n, h), kvq[:, h, :, 0:2 * D]).then_inc(s_st[h], 16)
                            sp.dma_start(rows_of(q_t, 0, n, h), kvq[:, h, :, 2 * D:3 * D]).then_inc(s_st[h], 16)
                        ahead(sp, load, store)
                        sp.wait_ge(s_st[0], 32 * (PAIRS + 1))
                        sp.wait_ge(s_st[1], 32 * PAIRS)

                    @block.gpsimd
                    def _(pool):
                        bound = pool.to_reg(ROWS - 1)
                        G.memset(hT[D:D + 1], 1.0).then_inc(s_one, 1)

                        def step(n, h):
                            pool.wait_ge(s_sl[h], 2 * n + 2)
                            pool.sem_inc(s_turn_p)
                            for j in range(J):
                                G.indirect_dma_start(
                                    out=info_t, out_offset=bass.IndirectOffsetOnAxis(ap=idx_s[:, h, j:j + 1], axis=0),
                                    in_=seg_s[:, h, j, :], in_offset=None, bounds_check=bound, oob_is_err=False
                                ).then_inc(s_sc[h], 16)
                        batches(pool, step)
                        s_sc.wait(pool, 0, 16 * J * (PAIRS + 1))
                        s_sc.wait(pool, 1, 16 * J * PAIRS)

                    @block.vector
                    def _(dve):
                        own = Own(dve, s_own, 2)

                        def early(n, h):
                            own.step(2 * n + h)
                            s_sc.wait(dve, h, 16 * J * n)
                            V.tensor_copy(idx_s[:, h, :], cols(seg_i, n, h)).then_inc(s_sl[h], 1)
                            V.tensor_copy(seg_s[:, h], cols(seg, n, h)).then_inc(s_sl[h], 1)
                            dve.wait_ge(s_x[h], 48 * (n + 1))
                            dve.wait_ge(s_h[h], n)
                            ln_vector(dve, own, n, h, xs[:, h], st, mv, rn, s_mv, s_sd, s_rn)
                            own.end()

                        def late(n, h):
                            dve.wait_ge(s_st[h], 32 * n)
                            for j in range(0, J, 2):
                                dve.wait_ge(s_om[j % 4][h], 2 * n + 1 + j // 4)
                                V.tensor_copy(kvq[:, h, j, :], ob[j % 4][:]).then_inc(s_oc[j % 4][h], 1)
                        ahead(dve, early, late)

                    @block.scalar
                    def _(act):
                        def early(n, h):
                            act.wait_ge(s_tp[1][h], n)
                            ln_scalar(act, n, h, xs[:, h], hh[:, h], mv, rn, s_mv, s_sd, s_rn,
                                      ACT.Relu).then_inc(s_h[h], 1)

                        def late(n, h):
                            for g in range(2):
                                act.wait_ge(s_tp[g][h], n + 1)
                                act.wait_ge(s_om[3][h], 2 * n)
                                A.copy(hT[0:D, h, g, :], tp[g][0:D, :]).then_inc(s_tc[g][h], 1)
                            act.wait_ge(s_st[h], 32 * n)
                            for j in range(1, J, 2):
                                act.wait_ge(s_om[j % 4][h], 2 * n + 1 + j // 4)
                                A.copy(kvq[:, h, j, :], ob[j % 4][:]).then_inc(s_oc[j % 4][h], 1)
                        ahead(act, early, late)

                    @block.tensor
                    def _(pe):
                        pe.wait_ge(s_one, 1)

                        def step(n, h):
                            pe.wait_ge(s_h[h], n + 1)
                            for g in range(2):
                                pe.wait_ge(s_tc[g][1 - h], n + h)
                                for j in range(4):
                                    last = T.transpose(tp[g][0:D, j * P:(j + 1) * P], hh[:, h, 4 * g + j, :], ident[:])
                                last.then_inc(s_tp[g][h], 1)
                            for j in range(J):
                                k = j % 4
                                if k == 0:
                                    pe.wait_ge(s_tc[j // 4][h], n + 1)
                                if j < 4:
                                    pe.wait_ge(s_oc[k][1 - h], 2 * n + 2 * h)
                                else:
                                    pe.wait_ge(s_oc[k][h], 2 * n + 1)
                                T.matmul(ob[k][:], hT[:, h, j // 4, k * P:(k + 1) * P], w_kvq[:],
                                         start=True, stop=True).then_inc(s_om[k][h], 1)
                        batches(pe, step)
        s_sc.close()
        retire()

        with ExitStack() as ph:
            info = sb("info", [P, CH, 4], F32, ph)
            no = sb("no", [P, CH], F32, ph)
            node_i = sb("node_i", [P, CH], I32, ph)
            node_f = sb("node_f", [P, CH], F32, ph)
            t0 = sb("t0", [P, CH], F32, ph)
            t1 = sb("t1", [P, CH], F32, ph)
            s_in, s_it, s_v, s_r, s_q = (sem("info_loaded"), sem("node_iota"), sem("info_vector"), sem("degrees_ready"),
                                         sem("degree_roots"))
            with nc.Block() as block:
                @block.sync
                def _(sp):
                    sp.dma_start(info[:], info_t.rearrange("(p j) d -> p j d", p=P)).then_inc(s_in, 16)

                @block.gpsimd
                def _(pool):
                    G.iota(node_i[:], [[1, CH]], base=0, channel_multiplier=CH).then_inc(s_it, 1)

                @block.scalar
                def _(act):
                    act.wait_ge(s_r, 2)
                    A.activation(root[:], t0[:], ACT.Sqrt).then_inc(s_q, 1)
                    A.activation(t1[:], t1[:], ACT.Sqrt).then_inc(s_q, 1)

                @block.vector
                def _(dve):
                    own = Own(dve, s_v)
                    dve.wait_ge(s_in, 16)
                    dve.wait_ge(s_it, 1)
                    V.tensor_scalar(t0[:], info[:, :, 1], 1.0, None, ALU.add).then_inc(s_r, 1)
                    own.add(V.tensor_copy(ptr_n[:], info[:, :, 0]))
                    own.add(V.tensor_copy(node_f[:], node_i[:]))
                    own.do(V.tensor_scalar(dinv[:], info[:, :, 2], 1.0, None, ALU.add))
                    V.tensor_scalar(t1[:], dinv[:], 1e-30, None, ALU.max).then_inc(s_r, 1)
                    own.add(V.tensor_copy(ptr_i[:], ptr_n[:]))
                    own.do(V.tensor_scalar(no[:], ptr_n[:], float(ZROW), None, ALU.is_equal))
                    pointers(own, ptr_n, no, node_f, info[:, :, 3], yptr_i, VALUES)
                    dve.wait_ge(s_q, 2)
                    own.add(V.reciprocal(iroot[:], root[:]))
                    own.add(V.reciprocal(t1[:], t1[:]))
                    own.do(V.tensor_scalar(dinv[:], dinv[:], 0.0, None, ALU.is_gt))
                    own.do(V.tensor_tensor(dinv[:], dinv[:], t1[:], ALU.mult))
        retire()

        with ExitStack() as p1:
            gkv = sb("e0_kv", [P, 2, J, 2 * D], F32, p1)
            gq = sb("e0_q", [P, 2, J, D], F32, p1)
            ea = sb("e0_ea", [P, 2, J, D], F32, p1)
            eaT = sb("e0_eaT", [D + 1, 2, 2, 4 * P], F32, p1)
            dst_s = sb("dst_s", [P, 2, J], I32, p1)
            g_ = sb("e0_g", [P, 2, J, WZ], F32, p1)
            S = sb("e0_S", [P, 2, J, WZ], F32, p1)
            sc = sb("e0_sc", [P, 2, J, HEADS], F32, p1)
            tp = [ps(f"e0_tp{g}", [P, 4 * P], p1) for g in range(2)]
            eo = [ps(f"e0_eo{g}", [P, 4, D], p1) for g in range(2)]
            pc = ps("e0_pc", [P, WZ], p1)
            s_ei, s_ix, s_gk, s_gq, s_rd, s_sc, s_ex, s_s, s_st = (
                sems("e0_ea_in"), sems("e0_rows_set"), s_stream[0], s_stream[1],
                sems("e0_msg_done"), sems("e0_scores"), sems("e0_exp"), sems("e0_sums"), sems("e0_stored"))
            s_tp = [sems(f"e0_tp{g}_full") for g in range(2)]
            s_tc = [sems(f"e0_tp{g}_copied") for g in range(2)]
            s_eo = [sems(f"e0_eo{g}_full") for g in range(2)]
            s_eu = [sems(f"e0_eo{g}_used") for g in range(2)]
            s_own, s_one, s_cr, s_z, s_zo = (sem("e0_vector"), sem("e0_ones"), sem("e0_carry"), sem("e0_first_sums"),
                                             sem("e0_first_stored"))

            with nc.Block() as block:
                @block.sync
                def _(sp):
                    def load(n, h):
                        sp.wait_ge(s_tp[1][h], n)
                        load_padded(sp, ea[:, h], edge_attr_96, e96_tail, n, h, s_ei[h])

                    def store(n, h):
                        sp.wait_ge(s_s[h], n + 1)
                        sp.dma_start(rows_of(agg0_t, 0, n, h), S[:, h]).then_inc(s_st[h], 16)
                    ahead(sp, load, store)
                    sp.wait_ge(s_z, 1)
                    sp.dma_start(agg0_t[AUX:AUX + P, :], Z[:]).then_inc(s_zo, 16)
                    sp.wait_ge(s_st[0], 16 * (PAIRS + 1))
                    sp.wait_ge(s_st[1], 16 * PAIRS)
                    sp.wait_ge(s_zo, 16)

                @block.gpsimd
                def _(pool):
                    G.memset(eaT[D:D + 1], 1.0).then_inc(s_one, 1)

                    def step(n, h):
                        pool.wait_ge(s_ix[h], 3 * n + 3)
                        pool.wait_ge(s_rd[h], n)
                        gathers(kv_t, lambda j: gkv[:, h, j, :], h, s_gk[h])
                        for j in range(J):
                            G.indirect_dma_start(out=gq[:, h, j, :], out_offset=None, in_=q_t,
                                                 in_offset=bass.IndirectOffsetOnAxis(ap=dst_s[:, h, j:j + 1], axis=0)
                                                 ).then_inc(s_gq[h], 16)
                    batches(pool, step)

                @block.tensor
                def _(pe):
                    pe.wait_ge(s_one, 1)

                    def step(n, h):
                        pe.wait_ge(s_ei[h], 48 * (n + 1))
                        for g in range(2):
                            pe.wait_ge(s_tc[g][1 - h], n + h)
                            for j in range(4):
                                last = T.transpose(tp[g][0:D, j * P:(j + 1) * P], ea[:, h, 4 * g + j, :], ident[:])
                            last.then_inc(s_tp[g][h], 1)
                        for g in range(2):
                            pe.wait_ge(s_tc[g][h], n + 1)
                            pe.wait_ge(s_eu[g][1 - h], n + h)
                            for j in range(4):
                                last = T.matmul(eo[g][:, j, :], eaT[:, h, g, j * P:(j + 1) * P], w_e[:],
                                                start=True, stop=True)
                            last.then_inc(s_eo[g][h], 1)
                    batches(pe, step)
                    pe.wait_ge(s_s[0], PAIRS + 1)
                    T.matmul(pc[:], B[:], S[:, 0, J - 1, :], start=True, stop=True).then_inc(s_cr, 1)

                @block.scalar
                def _(act):
                    def early(n, h):
                        s_gk.wait(act, h, 16 * J * n)
                        s_gq.wait(act, h, 16 * J * n)
                        act.wait_ge(s_s[h], n)
                        A.copy(idx_s[:, h, :], cols(src_i, n, h)).then_inc(s_ix[h], 1)
                        A.copy(dst_s[:, h, :], cols(dst_i, n, h)).then_inc(s_ix[h], 1)
                        A.copy(scan_s[:, h], cols(scan, n, h)).then_inc(s_ix[h], 1)

                    def late(n, h):
                        for g in range(2):
                            act.wait_ge(s_tp[g][h], n + 1)
                            act.wait_ge(s_eo[1][h], n)
                            A.copy(eaT[0:D, h, g, :], tp[g][0:D, :]).then_inc(s_tc[g][h], 1)
                        act.wait_ge(s_sc[h], n + 1)
                        A.activation(g_[:, h, :, D:WZ], sc[:, h], ACT.Exp).then_inc(s_ex[h], 1)
                    ahead(act, early, late)

                @block.vector
                def _(dve):
                    own = Own(dve, s_own, 6 + 2 * J - 1)
                    own.add(V.memset(S[:], 0.0))
                    own.do(V.memset(F[:], 0.0))
                    own.loop()

                    def step(n, h):
                        own.step(2 * n + h)
                        s_gk.wait(dve, h, 16 * J * (n + 1))
                        s_gq.wait(dve, h, 16 * J * (n + 1))
                        own.do(V.tensor_tensor(gq[:, h], gq[:, h], gkv[:, h, :, 0:D], ALU.mult))
                        for g in range(2):
                            dve.wait_ge(s_eo[g][h], n + 1)
                            V.tensor_tensor(gq[:, h, 4 * g:4 * g + 4, :], gq[:, h, 4 * g:4 * g + 4, :], eo[g][:],
                                            ALU.mult).then_inc(s_eu[g][h], 1)
                        dve.wait_ge(s_eu[1][h], n + 1)
                        own.do(V.reduce_sum(sc[:, h].rearrange("p j a -> p (j a)"),
                                            gq[:, h].rearrange("p j (a d) -> p (j a) d", d=HD), AX))
                        own.do(V.tensor_scalar(sc[:, h], sc[:, h], HD ** -0.5, -5.0, ALU.mult, ALU.max))
                        V.tensor_scalar(sc[:, h], sc[:, h], 5.0, None, ALU.min).then_inc(s_sc[h], 1)
                        dve.wait_ge(s_ex[h], n + 1)
                        for j in range(0, J, 2):
                            last = V.tensor_tensor(
                                g_[:, h, j:j + 2, 0:D].rearrange("p j (a d) -> p j a d", d=HD),
                                gkv[:, h, j:j + 2, D:2 * D].rearrange("p j (a d) -> p j a d", d=HD),
                                g_[:, h, j:j + 2, D:WZ].unsqueeze(3).to_broadcast([P, 2, HEADS, HD]), ALU.mult)
                            own.add(last) if j < J - 2 else last.then_inc(s_rd[h], 1)
                        dve.wait_ge(s_rd[h], n + 1)
                        own.settle()
                        dve.wait_ge(s_st[h], 16 * n)
                        scan_step(dve, own, n, h, WZ, g_[:, h], S, s_s, n + 1)
                        own.end()
                    batches(dve, step)
                    dve.wait_ge(s_cr, 1)
                    V.tensor_tensor(Z[:], F[:], pc[:], ALU.add).then_inc(s_z, 1)
        s_gk.close()
        s_gq.close()
        retire()

        with ExitStack() as p2:
            ag = sb("n1_ag", [P, 2, J, WZ], F32, p2)
            xs = sb("n1_x", [P, 2, J, D], F32, p2)
            rz = sb("n1_rz", [P, 2, J, HEADS], F32, p2)
            rec = sb("n1_rec", [P, 2, J, TR], F32, p2)
            st = sb("n1_st", [P, 2, J, 6], F32, p2)
            mv = sb("n1_mv", [P, 2, J, 2], F32, p2)
            rn = sb("n1_rn", [P, 2, 3, J], F32, p2)
            s_x, s_ix, s_g, s_x1, s_mv, s_sd, s_rn, s_h, s_st = (
                sems("n1_x_in"), sems("n1_rows_set"), s_stream[0], sems("n1_x_updated"),
                sems("n1_stats"), sems("n1_root"), sems("n1_scale"), sems("n1_h_ready"), sems("n1_stored"))
            s_own = sem("n1_vector")
            with nc.Block() as block:
                @block.sync
                def _(sp):
                    def load(n, h):
                        sp.wait_ge(s_st[h], 32 * n)
                        load_padded(sp, xs[:, h], x, x_tail, n, h, s_x[h])

                    def store(n, h):
                        sp.wait_ge(s_x1[h], n + 1)
                        sp.dma_start(rows_of(x1_t, 0, n, h), xs[:, h]).then_inc(s_st[h], 16)
                        sp.wait_ge(s_h[h], n + 1)
                        sp.dma_start(rows_of(rec_t, 0, n, h), rec[:, h]).then_inc(s_st[h], 16)
                    ahead(sp, load, store)
                    sp.wait_ge(s_st[0], 32 * (PAIRS + 1))
                    sp.wait_ge(s_st[1], 32 * PAIRS)

                @block.gpsimd
                def _(pool):
                    def step(n, h):
                        pool.wait_ge(s_ix[h], n + 1)
                        pool.wait_ge(s_x1[h], n)
                        gathers(agg0_t, lambda j: ag[:, h, j, :], h, s_g[h])
                    batches(pool, step)

                @block.vector
                def _(dve):
                    own = Own(dve, s_own, 5)

                    def step(n, h):
                        own.step(2 * n + h)
                        s_g.wait(dve, h, 16 * J * (n + 1))
                        own.do(V.tensor_scalar(rz[:, h], ag[:, h, :, D:WZ], 1e-6, None, ALU.add))
                        own.do(V.reciprocal(rz[:, h], rz[:, h]))
                        for j in range(0, J, 2):
                            v = ag[:, h, j:j + 2, 0:D].rearrange("p j (a d) -> p j a d", d=HD)
                            last = V.tensor_tensor(v, v, rz[:, h, j:j + 2, :].unsqueeze(3).to_broadcast(
                                [P, 2, HEADS, HD]), ALU.mult)
                        own.do(last)
                        dve.wait_ge(s_x[h], 48 * (n + 1))
                        V.tensor_tensor(xs[:, h], xs[:, h], ag[:, h, :, 0:D], ALU.add).then_inc(s_x1[h], 1)
                        dve.wait_ge(s_x1[h], n + 1)
                        dve.wait_ge(s_h[h], n)
                        ln_vector(dve, own, n, h, xs[:, h], st, mv, rn, s_mv, s_sd, s_rn)
                        own.end()
                    batches(dve, step)

                @block.scalar
                def _(act):
                    def early(n, h):
                        gather_slots(act, n, h, ptr_i, s_ix, s_g, 16 * J)

                    def late(n, h):
                        act.wait_ge(s_st[h], 32 * n)
                        A.copy(rec[:, h, :, D:TR], cols(ptr_n, n, h).unsqueeze(2))
                        ln_scalar(act, n, h, xs[:, h], rec[:, h, :, 0:D], mv, rn, s_mv, s_sd, s_rn,
                                  ACT.Relu).then_inc(s_h[h], 1)
                    ahead(act, early, late)
        s_g.close()
        retire()

        with ExitStack() as p3:
            xe = sb("e1_x", [P, 2, J, ED + TR], F32, p3)
            xT = sb("e1_xT", [P, 2, 2, 4 * P], F32, p3)
            mT = sb("e1_mT", [D + 1, 2, 2, 4 * P], F32, p3)
            gT = sb("e1_gT", [D + 1, 2, 2, 4 * P], F32, p3)
            gate = sb("e1_gate", [P, 2, J, 1], F32, p3)
            g_ = sb("e1_g", [P, 2, J, D], F32, p3)
            S = sb("e1_S", [P, 2, J, D], F32, p3)
            tp = [ps(f"e1_tp{g}", [P, 4 * P], p3) for g in range(2)]
            pm = ps("e1_pm", [P, 4 * P], p3)
            pg = ps("e1_pg", [P, 4 * P], p3)
            po = [ps(f"e1_po{g}", [P, 4, D + 1], p3) for g in range(2)]
            pc = ps("e1_pc", [P, D], p3)
            s_e, s_ix, s_g, s_pe, s_s, s_st = (sems("e1_ea_in"), sems("e1_rows_set"), s_stream[0],
                                               sems("e1_pointers_kept"), sems("e1_sums"), sems("e1_stored"))
            s_tp = [sems(f"e1_tp{g}_full") for g in range(2)]
            s_tc = [sems(f"e1_tp{g}_copied") for g in range(2)]
            s_pm, s_pg, s_mt, s_gt = sems("e1_pm_full"), sems("e1_pg_full"), sems("e1_m_gelu"), sems("e1_g_gelu")
            s_po = [sems(f"e1_po{g}_full") for g in range(2)]
            s_th = [sems(f"e1_gate{g}_tanh") for g in range(2)]
            s_pu = [sems(f"e1_po{g}_used") for g in range(2)]
            s_own, s_one, s_cr, s_z, s_zo = (sem("e1_vector"), sem("e1_ones"), sem("e1_carry"), sem("e1_first_sums"),
                                             sem("e1_first_stored"))
            with nc.Block() as block:
                @block.sync
                def _(sp):
                    def load(n, h):
                        sp.wait_ge(s_tp[1][h], n)
                        load_padded(sp, xe[:, h, :, 0:ED], edge_attr_32, e32_tail, n, h, s_e[h])

                    def store(n, h):
                        sp.wait_ge(s_s[h], n + 1)
                        sp.dma_start(rows_of(agg1_t, 0, n, h), S[:, h]).then_inc(s_st[h], 16)
                    ahead(sp, load, store)
                    sp.wait_ge(s_z, 1)
                    sp.dma_start(agg1_t[AUX:AUX + P, :], Z[:, 0:D]).then_inc(s_zo, 16)
                    sp.wait_ge(s_st[0], 16 * (PAIRS + 1))
                    sp.wait_ge(s_st[1], 16 * PAIRS)
                    sp.wait_ge(s_zo, 16)

                @block.gpsimd
                def _(pool):
                    G.memset(mT[D:D + 1], 1.0).then_inc(s_one, 1)
                    G.memset(gT[D:D + 1], 1.0).then_inc(s_one, 1)

                    def step(n, h):
                        pool.wait_ge(s_ix[h], 2 * n + 2)
                        pool.wait_ge(s_tp[1][h], n)
                        pool.wait_ge(s_pe[h], n)
                        gathers(rec_t, lambda j: xe[:, h, j, ED:ED + TR], h, s_g[h])
                    batches(pool, step)

                @block.tensor
                def _(pe):
                    pe.wait_ge(s_one, 2)

                    def early(n, h):
                        pe.wait_ge(s_e[h], 48 * (n + 1))
                        s_g.wait(pe, h, 16 * J * (n + 1))
                        for g in range(2):
                            pe.wait_ge(s_tc[g][1 - h], n + h)
                            for j in range(4):
                                last = T.transpose(tp[g][:, j * P:(j + 1) * P], xe[:, h, 4 * g + j, 0:P], ident[:])
                            last.then_inc(s_tp[g][h], 1)

                    def late(n, h):
                        for g in range(2):
                            pe.wait_ge(s_tc[g][h], n + 1)
                            for bank, w, full, used in ((pm, w_m1, s_pm, s_mt), (pg, w_g1, s_pg, s_gt)):
                                if g == 0:
                                    pe.wait_ge(used[1 - h], 2 * n + 2 * h)
                                else:
                                    pe.wait_ge(used[h], 2 * n + 1)
                                T.matmul(bank[0:D, :], w[:], xT[:, h, g, :], start=True, stop=True
                                         ).then_inc(full[h], 1)
                        for g in range(2):
                            pe.wait_ge(s_mt[h], 2 * n + 1 + g)
                            pe.wait_ge(s_gt[h], 2 * n + 1 + g)
                            pe.wait_ge(s_pu[g][1 - h], n + h)
                            for j in range(4):
                                c = slice(j * P, (j + 1) * P)
                                T.matmul(po[g][:, j, 0:D], mT[:, h, g, c], w_m2[:], start=True, stop=True)
                                last = T.matmul(po[g][:, j, D:D + 1], gT[:, h, g, c], w_g2[:], start=True, stop=True)
                            last.then_inc(s_po[g][h], 1)
                    ahead(pe, early, late)
                    pe.wait_ge(s_s[0], PAIRS + 1)
                    T.matmul(pc[:], B[:], S[:, 0, J - 1, :], start=True, stop=True).then_inc(s_cr, 1)

                @block.scalar
                def _(act):
                    def early(n, h):
                        act.wait_ge(s_s[h], n)
                        gather_slots(act, n, h, src_i, s_ix, s_g, 16 * J)
                        A.copy(scan_s[:, h], cols(scan, n, h)).then_inc(s_ix[h], 1)

                    def late(n, h):
                        s_g.wait(act, h, 16 * J * (n + 1))
                        A.copy(cols(ptr_e, n, h).unsqueeze(2), xe[:, h, :, ED + D:ED + TR]).then_inc(s_pe[h], 1)
                        for g in range(2):
                            act.wait_ge(s_tp[g][h], n + 1)
                            act.wait_ge(s_pg[h], 2 * n)
                            A.copy(xT[:, h, g, :], tp[g][:]).then_inc(s_tc[g][h], 1)
                        for g in range(2):
                            act.wait_ge(s_pm[h], 2 * n + 1 + g)
                            act.wait_ge(s_po[1][h], n)
                            A.activation(mT[0:D, h, g, :], pm[0:D, :], ACT.Gelu, bias=c_m1[:]).then_inc(s_mt[h], 1)
                            act.wait_ge(s_pg[h], 2 * n + 1 + g)
                            A.activation(gT[0:D, h, g, :], pg[0:D, :], ACT.Gelu, bias=c_g1[:]).then_inc(s_gt[h], 1)
                        for g in range(2):
                            act.wait_ge(s_po[g][h], n + 1)
                            act.wait_ge(s_pu[g][h], n)
                            A.activation(gate[:, h, 4 * g:4 * g + 4, :], po[g][:, :, D:D + 1], ACT.Tanh,
                                         scale=0.5).then_inc(s_th[g][h], 1)
                    ahead(act, early, late)

                @block.vector
                def _(dve):
                    own = Own(dve, s_own, 2 + 2 * J - 1)
                    own.add(V.memset(S[:], 0.0))
                    own.do(V.memset(F[:], 0.0))
                    own.loop()

                    def step(n, h):
                        own.step(2 * n + h)
                        for g in range(2):
                            c = slice(4 * g, 4 * g + 4)
                            dve.wait_ge(s_th[g][h], n + 1)
                            own.do(V.tensor_scalar(gate[:, h, c, :], gate[:, h, c, :], 0.5, 0.5, ALU.mult, ALU.add))
                            V.tensor_tensor(g_[:, h, c, :], po[g][:, :, 0:D], gate[:, h, c, :].to_broadcast([P, 4, D]),
                                            ALU.mult).then_inc(s_pu[g][h], 1)
                        for g in range(2):
                            dve.wait_ge(s_pu[g][h], n + 1)
                        dve.wait_ge(s_ix[h], 2 * n + 2)
                        dve.wait_ge(s_st[h], 16 * n)
                        scan_step(dve, own, n, h, D, g_[:, h], S, s_s, n + 1)
                        own.end()
                    batches(dve, step)
                    dve.wait_ge(s_cr, 1)
                    V.tensor_tensor(Z[:, 0:D], F[:, 0:D], pc[:], ALU.add).then_inc(s_z, 1)
        s_g.close()
        retire()

        with ExitStack() as p4:
            ag = sb("n2_ag", [P, 2, J, D], F32, p4)
            rec = sb("n2_rec", [P, 2, J, TR], F32, p4)
            x1 = sb("n2_x1", [P, 2, J, D], F32, p4)
            rT = sb("n2_rT", [D, 2, 2, 4 * P], F32, p4)
            aT = sb("n2_aT", [D, 2, 2, 4 * P], F32, p4)
            uT = sb("n2_uT", [D + 1, 2, 2, 4 * P], F32, p4)
            hs = sb("n2_h", [P, 2, J, D], F32, p4)
            ln = sb("n2_ln", [P, 2, J, D], F32, p4)
            x2 = sb("n2_x2", [P, 2, J, D], F32, p4)
            y0 = sb("n2_y0", [P, 2, J, D], F32, p4)
            st = sb("n2_st", [P, 2, J, 6], F32, p4)
            mv = sb("n2_mv", [P, 2, J, 2], F32, p4)
            rn = sb("n2_rn", [P, 2, 3, J], F32, p4)
            mv2 = sb("n2_mv2", [P, 2, J, 2], F32, p4)
            rn2 = sb("n2_rn2", [P, 2, 3, J], F32, p4)
            tr = ps("n2_tr", [P, 4 * P], p4)
            ta = ps("n2_ta", [P, 4 * P], p4)
            pu = [ps(f"n2_pu{g}", [P, 4 * P], p4) for g in range(2)]
            po = [ps(f"n2_po{g}", [P, 4, D], p4) for g in range(2)]
            s_r, s_x, s_ix, s_g, s_st = (sems("n2_rec_in"), sems("n2_x1_in"), sems("n2_rows_set"), s_stream[0],
                                         sems("n2_stored"))
            s_tr, s_ta, s_cr_, s_ca = (sems("n2_tr_full"), sems("n2_ta_full"), sems("n2_tr_copied"),
                                       sems("n2_ta_copied"))
            s_pu, s_ut, s_po, s_hs = sems("n2_pu_full"), sems("n2_gelu"), sems("n2_po_full"), sems("n2_h_ready")
            s_mv, s_sd, s_rn, s_ln = sems("n2_stats"), sems("n2_root"), sems("n2_scale"), sems("n2_ln_ready")
            s_x2, s_mv2, s_sd2, s_rn2, s_sn, s_y0 = (sems("n2_x2_ready"), sems("n2_stats2"), sems("n2_root2"),
                                                     sems("n2_scale2"), sems("n2_scale2_by_degree"), sems("n2_y0_ready"))
            s_own, s_one = sem("n2_vector"), sem("n2_ones")
            with nc.Block() as block:
                @block.sync
                def _(sp):
                    def load(n, h):
                        sp.wait_ge(s_hs[h], 2 * n)
                        sp.dma_start(rec[:, h], rows_of(rec_t, 0, n, h)).then_inc(s_r[h], 16)
                        sp.wait_ge(s_x2[h], n)
                        sp.dma_start(x1[:, h], rows_of(x1_t, 0, n, h)).then_inc(s_x[h], 16)

                    def store(n, h):
                        sp.wait_ge(s_x2[h], n + 1)
                        sp.dma_start(rows_of(x2_t, 0, n, h), x2[:, h]).then_inc(s_st[h], 16)
                        sp.wait_ge(s_y0[h], n + 1)
                        for t in y_t:
                            sp.dma_start(rows_of(t, 0, n, h), y0[:, h]).then_inc(s_st[h], 16)
                    ahead(sp, load, store)
                    sp.wait_ge(s_st[0], 48 * (PAIRS + 1))
                    sp.wait_ge(s_st[1], 48 * PAIRS)

                @block.gpsimd
                def _(pool):
                    G.memset(uT[D:D + 1], 1.0).then_inc(s_one, 1)

                    def step(n, h):
                        pool.wait_ge(s_ix[h], n + 1)
                        pool.wait_ge(s_ta[h], 2 * n)
                        gathers(agg1_t, lambda j: ag[:, h, j, :], h, s_g[h])
                    batches(pool, step)

                @block.tensor
                def _(pe):
                    pe.wait_ge(s_one, 1)

                    def early(n, h):
                        pe.wait_ge(s_r[h], 16 * (n + 1))
                        s_g.wait(pe, h, 16 * J * (n + 1))
                        for g in range(2):
                            for bank, rows, full, used in ((tr, rec, s_tr, s_cr_), (ta, ag, s_ta, s_ca)):
                                if g == 0:
                                    pe.wait_ge(used[1 - h], 2 * n + 2 * h)
                                else:
                                    pe.wait_ge(used[h], 2 * n + 1)
                                for j in range(4):
                                    last = T.transpose(bank[0:D, j * P:(j + 1) * P], rows[:, h, 4 * g + j, 0:D],
                                                       ident[:])
                                last.then_inc(full[h], 1)

                    def late(n, h):
                        for g in range(2):
                            pe.wait_ge(s_cr_[h], 2 * n + 1 + g)
                            pe.wait_ge(s_ca[h], 2 * n + 1 + g)
                            pe.wait_ge(s_ut[1 - h], 2 * n + 2 * h)
                            T.matmul(pu[g][0:D, :], w_ua[:], rT[:, h, g, :], start=True, stop=False)
                            T.matmul(pu[g][0:D, :], w_ub[:], aT[:, h, g, :], start=False, stop=True
                                     ).then_inc(s_pu[h], 1)
                        for g in range(2):
                            pe.wait_ge(s_ut[h], 2 * n + 1 + g)
                            pe.wait_ge(s_hs[1 - h], 2 * n + 2 * h)
                            for j in range(4):
                                last = T.matmul(po[g][:, j, :], uT[:, h, g, j * P:(j + 1) * P], w_u2[:],
                                                start=True, stop=True)
                            last.then_inc(s_po[h], 1)
                    ahead(pe, early, late)

                @block.scalar
                def _(act):
                    def early(n, h):
                        gather_slots(act, n, h, ptr_i, s_ix, s_g, 16 * J)
                        for g in range(2):
                            act.wait_ge(s_tr[h], 2 * n + 1 + g)
                            act.wait_ge(s_pu[h], 2 * n)
                            A.copy(rT[:, h, g, :], tr[0:D, :]).then_inc(s_cr_[h], 1)

                    def late(n, h):
                        for g in range(2):
                            act.wait_ge(s_pu[h], 2 * n + 1 + g)
                            act.wait_ge(s_po[h], 2 * n)
                            A.activation(uT[0:D, h, g, :], pu[g][0:D, :], ACT.Gelu, bias=c_u1[:]).then_inc(s_ut[h], 1)
                        act.wait_ge(s_x2[h], n)
                        ln_scalar(act, n, h, hs[:, h], ln[:, h], mv, rn, s_mv, s_sd, s_rn,
                                  ACT.Identity).then_inc(s_ln[h], 1)
                        act.wait_ge(s_mv2[h], n + 1)
                        A.activation(rn2[:, h, 2, :], mv2[:, h, :, 1], ACT.Sqrt, bias=eps[:]).then_inc(s_sd2[h], 1)
                        act.wait_ge(s_st[h], 48 * n)
                        act.wait_ge(s_sn[h], n + 1)
                        for j in range(J):
                            last = A.activation(y0[:, h, j, :], x2[:, h, j, :], ACT.Relu, scale=rn2[:, h, 0, j:j + 1],
                                                bias=rn2[:, h, 1, j:j + 1])
                        last.then_inc(s_y0[h], 1)
                    ahead(act, early, late)

                @block.vector
                def _(dve):
                    own = Own(dve, s_own, 2 + 2 + 2 + 1)

                    def early(n, h):
                        for g in range(2):
                            dve.wait_ge(s_ta[h], 2 * n + 1 + g)
                            dve.wait_ge(s_pu[h], 2 * n)
                            V.tensor_copy(aT[:, h, g, :], ta[0:D, :]).then_inc(s_ca[h], 1)

                    def late(n, h):
                        own.step(2 * n + h)
                        dve.wait_ge(s_ln[h], n)
                        for g in range(2):
                            c = slice(4 * g, 4 * g + 4)
                            dve.wait_ge(s_po[h], 2 * n + 1 + g)
                            V.tensor_tensor(hs[:, h, c, :], rec[:, h, c, 0:D], po[g][:], ALU.add).then_inc(s_hs[h], 1)
                        dve.wait_ge(s_hs[h], 2 * n + 2)
                        ln_vector(dve, own, n, h, hs[:, h], st, mv, rn, s_mv, s_sd, s_rn)
                        dve.wait_ge(s_x[h], 16 * (n + 1))
                        dve.wait_ge(s_st[h], 48 * n)
                        own.add(V.tensor_tensor(x2[:, h], x1[:, h], r_all[:, 1:2, :].to_broadcast([P, J, D]), ALU.add))
                        dve.wait_ge(s_ln[h], n + 1)
                        own.do(V.tensor_tensor(ln[:, h], ln[:, h], r_all[:, 0:1, :].to_broadcast([P, J, D]), ALU.mult))
                        V.tensor_tensor(x2[:, h], x2[:, h], ln[:, h], ALU.add).then_inc(s_x2[h], 1)
                        dve.wait_ge(s_x2[h], n + 1)
                        dve.wait_ge(s_y0[h], n)
                        ln_vector(dve, own, n, h, x2[:, h], st, mv2, rn2, s_mv2, s_sd2, s_rn2)
                        dve.wait_ge(s_rn2[h], n + 1)
                        own.add(V.tensor_tensor(rn2[:, h, 0, :], rn2[:, h, 0, :], cols(iroot, n, h), ALU.mult))
                        V.tensor_tensor(rn2[:, h, 1, :], rn2[:, h, 1, :], cols(iroot, n, h), ALU.mult
                                        ).then_inc(s_sn[h], 1)
                        own.settle()
                    ahead(dve, early, late)
        s_g.close()
        retire()

        with ExitStack() as p5:
            H = sb("H", [P, CH, D], F32, p5)
            g_ = sb("r_g", [P, 2, J, D], F32, p5)
            cs = sb("r_c", [P, 2, J, D], F32, p5)
            S = sb("r_S", [P, 2, J, D], F32, p5)
            z0 = sb("r_z0", [P, D], F32, p5)
            zs = sb("r_zs", [P, D], F32, p5)
            zc = sb("r_zc", [P, D], F32, p5)
            idx_z = sb("idx_z", [P, 1], I32, p5)
            t_ = sb("r_t", [P, CH], F32, p5)
            yptr_e = sb("yptr_e", [P, CH], I32, p5)
            dst_s = sb("r_dst_s", [P, 2, J], I32, p5)
            pc = ps("r_pc", [P, D], p5)
            k_wide = lambda n, h: cols(k_e, n, h).unsqueeze(2).to_broadcast([P, J, D])

            def update(dve, own, n, h, signal):
                v = cols(H, n, h)
                own.do(V.tensor_tensor(v, v, k_wide(n, h), ALU.mult))
                V.scalar_tensor_tensor(out=v, in0=cs[:, h], scalar=ALPHA, in1=v, op0=ALU.mult,
                                       op1=ALU.add).then_inc(signal, 1)

            def finish_round(dve, own, s_cr, count, before, s_z):
                dve.wait_ge(s_cr, count)
                own.do(V.tensor_tensor(Z[:, 0:D], F[:, 0:D], pc[:], ALU.add))
                own.add(V.memset(F[:], 0.0))
                own.do(V.tensor_tensor(Z[:, 0:D], Z[:, 0:D], before[:], ALU.add))
                V.scalar_tensor_tensor(out=zs[:], in0=Z[:, 0:D], scalar=k_z[:], in1=z0[:], op0=ALU.mult,
                                       op1=ALU.add).then_inc(s_z, 1)

            s_v, s_ix, s_g, s_c, s_s, s_st, s_ct = (
                sem("r1_vector"), sems("r1_rows_set"), s_stream[0], s_stream[1], sems("r1_values"), sems("r1_stored"), sems("r1_start_stored"))
            s_cr, s_z, s_zo, s_c0, s_i0 = (sem("r1_carry"), sem("r1_first_values"), sem("r1_first_stored"),
                                           s_single, sem("r1_first_rows"))
            with nc.Block() as block:
                @block.sync
                def _(sp):
                    def step(n, h):
                        s_c.wait(sp, h, 16 * J * (n + 1))
                        sp.dma_start(rows_of(c_t, 0, n, h), cs[:, h]).then_inc(s_ct[h], 16)
                        sp.wait_ge(s_s[h], n + 1)
                        sp.sem_inc(s_turn_s)
                        sp.dma_start(rows_of(y_t[0], VALUES, n, h), cols(H, n, h)).then_inc(s_st[h], 16)
                    batches(sp, step)
                    sp.wait_ge(s_z, 1)
                    sp.dma_start(y_t[0][VALUES + AUX:VALUES + AUX + P, :], zs[:]).then_inc(s_zo, 16)
                    for s in (s_ct, s_st):
                        sp.wait_ge(s[0], 16 * (PAIRS + 1))
                        sp.wait_ge(s[1], 16 * PAIRS)
                    sp.wait_ge(s_zo, 16)

                @block.gpsimd
                def _(pool):
                    pool.wait_ge(s_i0, 1)
                    G.indirect_dma_start(out=zc[:], out_offset=None, in_=y_t[0][0:ROWS, :],
                                         in_offset=bass.IndirectOffsetOnAxis(ap=idx_z[:], axis=0)).then_inc(s_c0, 16)

                    def step(n, h):
                        pool.wait_ge(s_ix[h], 3 * n + 3)
                        pool.wait_ge(s_s[h], n)
                        pool.wait_ge(s_ct[h], 16 * n)
                        gathers(y_t[0][0:ROWS, :], lambda j: g_[:, h, j, :], h, s_g[h])
                        for j in range(J):
                            G.indirect_dma_start(out=cs[:, h, j, :], out_offset=None, in_=y_t[0][0:ROWS, :],
                                                 in_offset=bass.IndirectOffsetOnAxis(ap=dst_s[:, h, j:j + 1], axis=0)
                                                 ).then_inc(s_c[h], 16)
                    batches(pool, step)

                @block.tensor
                def _(pe):
                    pe.wait_ge(s_s[0], PAIRS + 1)
                    T.matmul(pc[:], B[:], S[:, 0, J - 1, :], start=True, stop=True).then_inc(s_cr, 1)

                @block.scalar
                def _(act):
                    A.copy(idx_z[:], dst_i[:, 0:1]).then_inc(s_i0, 1)

                    def step(n, h):
                        s_g.wait(act, h, 16 * J * n)
                        s_c.wait(act, h, 16 * J * n)
                        act.wait_ge(s_s[h], n)
                        A.copy(idx_s[:, h, :], cols(src_i, n, h)).then_inc(s_ix[h], 1)
                        A.copy(dst_s[:, h, :], cols(dst_i, n, h)).then_inc(s_ix[h], 1)
                        A.copy(scan_s[:, h], cols(scan, n, h)).then_inc(s_ix[h], 1)
                    batches(act, step)

                @block.vector
                def _(dve):
                    own = Own(dve, s_v, 2 * J + 2)
                    own.add(V.memset(S[:], 0.0))
                    own.do(V.memset(F[:], 0.0))
                    t = H[:, 0:5, :].rearrange("p a d -> p (a d)")[:, 0:CH]
                    no = H[:, 5:10, :].rearrange("p a d -> p (a d)")[:, 0:CH]
                    own.add(V.tensor_scalar(no, ptr_e[:], float(ZROW), None, ALU.is_equal))
                    own.do(V.tensor_copy(t, src_i[:]))
                    pointers(own, ptr_e, no, t, t_[:], yptr_e, VALUES)
                    own.settle()
                    dve.wait_ge(s_c0, 16)
                    own.do(V.tensor_scalar(z0[:], zc[:], ALPHA, None, ALU.mult))
                    own.loop()

                    def step(n, h):
                        own.step(2 * n + h)
                        s_g.wait(dve, h, 16 * J * (n + 1))
                        scan_step(dve, own, n, h, D, g_[:, h], S)
                        s_c.wait(dve, h, 16 * J * (n + 1))
                        v = cols(H, n, h)
                        own.do(V.tensor_tensor(v, S[:, h], cs[:, h], ALU.add))
                        update(dve, own, n, h, s_s[h])
                        own.end()

                    batches(dve, step)
                    finish_round(dve, own, s_cr, 1, zc, s_z)
            s_g.close()
            s_c.close()
            retire()

            s_v, s_ix, s_g, s_c, s_s, s_st = (sem("r_vector"), sems("r_rows_set"), s_stream[2],
                                              sems("r_start_loaded"), sems("r_values"), sems("r_stored"))
            s_cr, s_z, s_zo = sem("r_carry"), sem("r_first_values"), sem("r_first_stored")
            PER = [PAIRS + 1, PAIRS]

            def rounds(eng, one):
                one(0, 0)
                with eng.Fori(0, ROUNDS // 2 - 1) as q:
                    one(2 * q + 1, 1)
                    one(2 * q + 2, 0)

            def pass_of(eng, r, step):
                batches(eng, lambda n, h: step(r * PER[h] + n, n, h))

            with nc.Block() as block:
                @block.sync
                def _(sp):
                    def one(r, odd):
                        to = y_t[1 - odd]

                        def step(m, n, h):
                            sp.wait_ge(s_s[h], m + 1)
                            sp.sem_inc(s_turn_s)
                            sp.dma_start(rows_of(to, VALUES, n, h), cols(H, n, h)).then_inc(s_st[h], 16)
                        pass_of(sp, r, step)
                        sp.wait_ge(s_z, r + 1)
                        sp.dma_start(to[VALUES + AUX:VALUES + AUX + P, :], zs[:]).then_inc(s_zo, 16)
                    rounds(sp, one)
                    for h in range(2):
                        sp.wait_ge(s_st[h], 16 * (ROUNDS - 1) * PER[h])
                    sp.wait_ge(s_zo, 16 * (ROUNDS - 1))

                @block.gpsimd
                def _(pool):
                    def one(r, odd):
                        pool.wait_ge(s_st[0], 16 * PER[0] * r)
                        pool.wait_ge(s_st[1], 16 * PER[1] * r)
                        pool.wait_ge(s_zo, 16 * r)
                        pool.sem_inc(s_turn_p)

                        def step(m, n, h):
                            pool.wait_ge(s_ix[h], 2 * m + 2)
                            pool.wait_ge(s_s[h], m)
                            gathers(y_t[odd], lambda j: g_[:, h, j, :], h, s_g[h])
                        pass_of(pool, r, step)
                    rounds(pool, one)

                @block.tensor
                def _(pe):
                    def one(r, odd):
                        pe.wait_ge(s_s[0], PER[0] * (r + 1))
                        T.matmul(pc[:], B[:], S[:, 0, J - 1, :], start=True, stop=True).then_inc(s_cr, 1)
                    rounds(pe, one)

                @block.scalar
                def _(act):
                    def one(r, odd):
                        def step(m, n, h):
                            act.wait_ge(s_s[h], m)
                            act.dma_start(cs[:, h], rows_of(c_t, 0, n, h)).then_inc(s_c[h], 16)
                            gather_slots(act, m, h, yptr_e, s_ix, s_g, 16 * J, n)
                            A.copy(scan_s[:, h], cols(scan, n, h)).then_inc(s_ix[h], 1)
                        pass_of(act, r, step)
                    rounds(act, one)

                @block.vector
                def _(dve):
                    own = Own(dve, s_v)
                    per_batch = 2 * J + 2
                    per_round = NB * per_batch + 3

                    def one(r, odd):
                        def step(m, n, h):
                            own.base, own.n = r * per_round + (2 * n + h) * per_batch, 0
                            dve.wait_ge(s_ix[h], 2 * m + 2)
                            s_g.wait(dve, h, 16 * J * (m + 1))
                            scan_step(dve, own, n, h, D, g_[:, h], S)
                            v = cols(H, n, h)
                            own.do(V.tensor_tensor(v, v, S[:, h], ALU.add))
                            dve.wait_ge(s_c[h], 16 * (m + 1))
                            update(dve, own, n, h, s_s[h])
                            assert own.n == per_batch
                        pass_of(dve, r, step)
                        own.base, own.n = r * per_round + NB * per_batch, 0
                        finish_round(dve, own, s_cr, r + 1, zs, s_z)
                        assert own.n == 3
                        dve.wait_ge(s_z, r + 1)
                        dve.sem_inc(s_turn_v)
                    rounds(dve, one)
        s_g.close(ROUNDS - 1)
        retire()

        with ExitStack() as p6:
            yg = sb("n3_y", [P, 2, J, D], F32, p6)
            xs = sb("n3_x", [P, 2, J, D], F32, p6)
            h3 = sb("n3_h", [P, 2, J, D], F32, p6)
            hT = sb("n3_hT", [D, 2, 2, 4 * P], F32, p6)
            zt = sb("n3_z", [P, 2, J, D], F32, p6)
            st = sb("n3_st", [P, 2, J, 6], F32, p6)
            mv = sb("n3_mv", [P, 2, J, 2], F32, p6)
            rn = sb("n3_rn", [P, 2, 3, J], F32, p6)
            tp = [ps(f"n3_tp{g}", [P, 4 * P], p6) for g in range(2)]
            po = [ps(f"n3_po{g}", [P, 4, D], p6) for g in range(2)]
            s_x, s_ix, s_g, s_x3, s_mv, s_sd, s_rn, s_h, s_st = (
                sems("n3_x_in"), sems("n3_rows_set"), s_stream[0], sems("n3_x_updated"), sems("n3_stats"),
                sems("n3_root"), sems("n3_scale"), sems("n3_h_ready"), sems("n3_stored"))
            s_tp = [sems(f"n3_tp{g}_full") for g in range(2)]
            s_tc = [sems(f"n3_tp{g}_copied") for g in range(2)]
            s_po = [sems(f"n3_po{g}_full") for g in range(2)]
            s_pu = [sems(f"n3_po{g}_used") for g in range(2)]
            s_own = sem("n3_vector")
            with nc.Block() as block:
                @block.sync
                def _(sp):
                    def load(n, h):
                        sp.wait_ge(s_st[h], 32 * n)
                        sp.wait_ge(s_h[h], n)
                        sp.dma_start(xs[:, h], rows_of(x2_t, 0, n, h)).then_inc(s_x[h], 16)

                    def store(n, h):
                        sp.wait_ge(s_x3[h], n + 1)
                        sp.dma_start(rows_of(x3_t, 0, n, h), xs[:, h]).then_inc(s_st[h], 16)
                        for g in range(2):
                            sp.wait_ge(s_pu[g][h], n + 1)
                        sp.dma_start(rows_of(z_t, 0, n, h), zt[:, h]).then_inc(s_st[h], 16)
                    ahead(sp, load, store)
                    sp.wait_ge(s_st[0], 32 * (PAIRS + 1))
                    sp.wait_ge(s_st[1], 32 * PAIRS)

                @block.gpsimd
                def _(pool):
                    def step(n, h):
                        pool.wait_ge(s_ix[h], n + 1)
                        pool.wait_ge(s_x3[h], n)
                        gathers(y_t[1], lambda j: yg[:, h, j, :], h, s_g[h])
                    batches(pool, step)

                @block.vector
                def _(dve):
                    own = Own(dve, s_own, 3)

                    def early(n, h):
                        own.step(2 * n + h)
                        s_g.wait(dve, h, 16 * J * (n + 1))
                        own.do(V.tensor_tensor(yg[:, h], yg[:, h], cols(root, n, h).unsqueeze(2).to_broadcast([P, J, D]),
                                               ALU.mult))
                        dve.wait_ge(s_x[h], 16 * (n + 1))
                        V.tensor_tensor(xs[:, h], xs[:, h], yg[:, h], ALU.add).then_inc(s_x3[h], 1)
                        dve.wait_ge(s_x3[h], n + 1)
                        dve.wait_ge(s_h[h], n)
                        ln_vector(dve, own, n, h, xs[:, h], st, mv, rn, s_mv, s_sd, s_rn)
                        own.end()

                    def late(n, h):
                        dve.wait_ge(s_st[h], 32 * n)
                        for g in range(2):
                            c = slice(4 * g, 4 * g + 4)
                            dve.wait_ge(s_po[g][h], n + 1)
                            V.tensor_tensor(zt[:, h, c, :], po[g][:],
                                            cols(dinv, n, h)[:, c].unsqueeze(2).to_broadcast([P, 4, D]),
                                            ALU.mult).then_inc(s_pu[g][h], 1)
                    ahead(dve, early, late)

                @block.scalar
                def _(act):
                    def early(n, h):
                        gather_slots(act, n, h, yptr_i, s_ix, s_g, 16 * J)
                        act.wait_ge(s_tp[1][h], n)
                        ln_scalar(act, n, h, xs[:, h], h3[:, h], mv, rn, s_mv, s_sd, s_rn,
                                  ACT.Relu).then_inc(s_h[h], 1)

                    def late(n, h):
                        for g in range(2):
                            act.wait_ge(s_tp[g][h], n + 1)
                            act.wait_ge(s_po[1][h], n)
                            A.copy(hT[:, h, g, :], tp[g][0:D, :]).then_inc(s_tc[g][h], 1)
                    ahead(act, early, late)

                @block.tensor
                def _(pe):
                    def step(n, h):
                        pe.wait_ge(s_h[h], n + 1)
                        for g in range(2):
                            pe.wait_ge(s_tc[g][1 - h], n + h)
                            for j in range(4):
                                last = T.transpose(tp[g][0:D, j * P:(j + 1) * P], h3[:, h, 4 * g + j, :], ident[:])
                            last.then_inc(s_tp[g][h], 1)
                        for g in range(2):
                            pe.wait_ge(s_tc[g][h], n + 1)
                            pe.wait_ge(s_pu[g][1 - h], n + h)
                            for j in range(4):
                                last = T.matmul(po[g][:, j, :], hT[:, h, g, j * P:(j + 1) * P], w_3[:],
                                                start=True, stop=True)
                            last.then_inc(s_po[g][h], 1)
                    batches(pe, step)
        s_g.close()
        retire()

        with ExitStack() as p7:
            g_ = sb("e3_g", [P, 2, J, D], F32, p7)
            S = sb("e3_S", [P, 2, J, D], F32, p7)
            pc = ps("e3_pc", [P, D], p7)
            s_ix, s_g, s_s, s_st = sems("e3_rows_set"), s_stream[0], sems("e3_sums"), sems("e3_stored")
            s_own, s_cr, s_z, s_zo = sem("e3_vector"), sem("e3_carry"), sem("e3_first_sums"), sem("e3_first_stored")
            with nc.Block() as block:
                @block.sync
                def _(sp):
                    def step(n, h):
                        sp.wait_ge(s_s[h], n + 1)
                        sp.dma_start(rows_of(agg3_t, 0, n, h), S[:, h]).then_inc(s_st[h], 16)
                    batches(sp, step)
                    sp.wait_ge(s_z, 1)
                    sp.dma_start(agg3_t[AUX:AUX + P, :], Z[:, 0:D]).then_inc(s_zo, 16)
                    sp.wait_ge(s_st[0], 16 * (PAIRS + 1))
                    sp.wait_ge(s_st[1], 16 * PAIRS)
                    sp.wait_ge(s_zo, 16)

                @block.gpsimd
                def _(pool):
                    def step(n, h):
                        pool.wait_ge(s_ix[h], 2 * n + 2)
                        pool.wait_ge(s_s[h], n)
                        gathers(z_t, lambda j: g_[:, h, j, :], h, s_g[h])
                    batches(pool, step)

                @block.tensor
                def _(pe):
                    pe.wait_ge(s_s[0], PAIRS + 1)
                    T.matmul(pc[:], B[:], S[:, 0, J - 1, :], start=True, stop=True).then_inc(s_cr, 1)

                @block.scalar
                def _(act):
                    def step(n, h):
                        act.wait_ge(s_s[h], n)
                        gather_slots(act, n, h, src_i, s_ix, s_g, 16 * J)
                        A.copy(scan_s[:, h], cols(scan, n, h)).then_inc(s_ix[h], 1)
                    batches(act, step)

                @block.vector
                def _(dve):
                    own = Own(dve, s_own, 1 + 2 * J - 1)
                    own.add(V.memset(S[:], 0.0))
                    own.do(V.memset(F[:], 0.0))
                    own.loop()

                    def step(n, h):
                        own.step(2 * n + h)
                        dve.wait_ge(s_ix[h], 2 * n + 2)
                        s_g.wait(dve, h, 16 * J * (n + 1))
                        own.do(V.tensor_tensor(g_[:, h], g_[:, h], scan_s[:, h, :, 2:3].to_broadcast([P, J, D]),
                                               ALU.mult))
                        dve.wait_ge(s_st[h], 16 * n)
                        scan_step(dve, own, n, h, D, g_[:, h], S, s_s, n + 1)
                        own.end()
                    batches(dve, step)
                    dve.wait_ge(s_cr, 1)
                    V.tensor_tensor(Z[:, 0:D], F[:, 0:D], pc[:], ALU.add).then_inc(s_z, 1)
        s_g.close()
        retire()

        with ExitStack() as p8:
            ag = sb("n4_ag", [P, 2, J, D], F32, p8)
            zt = sb("n4_z", [P, 2, J, D], F32, p8)
            xs = sb("n4_x", [P, 2, J, D], F32, p8)
            o_ = sb("n4_o", [P, 2, J, D], F32, p8)
            s_x, s_ix, s_g, s_o, s_st = (sems("n4_in"), sems("n4_rows_set"), s_stream[0], sems("n4_out"),
                                         sems("n4_stored"))
            s_own, s_t = sem("n4_vector"), sem("n4_tail_stored")
            out_v = out[0:FULL * CH, :].rearrange("(p j) d -> p j d", j=CH)
            with nc.Block() as block:
                @block.sync
                def _(sp):
                    def load(n, h):
                        sp.wait_ge(s_o[h], n)
                        sp.dma_start(zt[:, h], rows_of(z_t, 0, n, h)).then_inc(s_x[h], 16)
                        sp.dma_start(xs[:, h], rows_of(x3_t, 0, n, h)).then_inc(s_x[h], 16)

                    def store(n, h):
                        sp.wait_ge(s_o[h], n + 1)
                        c = bass.ds((2 * n + h) * J, J)
                        sp.dma_start(out_v[0:SPLIT, c, :], o_[0:SPLIT, h]).then_inc(s_st[h], 16)
                        sp.dma_start(out_v[SPLIT:FULL, c, :], o_[SPLIT:FULL, h]).then_inc(s_st[h], 16)
                        sp.dma_start(out_tail.rearrange("(a j) d -> a j d", a=1)[:, c, :], o_[FULL:P, h]
                                     ).then_inc(s_st[h], 16)
                    ahead(sp, load, store)
                    sp.wait_ge(s_st[0], 48 * (PAIRS + 1))
                    sp.wait_ge(s_st[1], 48 * PAIRS)
                    sp.dma_start(out[FULL * CH:N, :], out_tail[0:TAIL, :]).then_inc(s_t, 16)
                    sp.wait_ge(s_t, 16)

                @block.gpsimd
                def _(pool):
                    def step(n, h):
                        pool.wait_ge(s_ix[h], n + 1)
                        pool.wait_ge(s_o[h], n)
                        gathers(agg3_t, lambda j: ag[:, h, j, :], h, s_g[h])
                    batches(pool, step)

                @block.scalar
                def _(act):
                    def step(n, h):
                        gather_slots(act, n, h, ptr_i, s_ix, s_g, 16 * J)
                    batches(act, step)

                @block.vector
                def _(dve):
                    own = Own(dve, s_own, 3)

                    def step(n, h):
                        own.step(2 * n + h)
                        dve.wait_ge(s_x[h], 32 * (n + 1))
                        own.add(V.tensor_tensor(xs[:, h], xs[:, h], r_all[:, 2:3, :].to_broadcast([P, J, D]), ALU.add))
                        s_g.wait(dve, h, 16 * J * (n + 1))
                        own.do(V.tensor_tensor(ag[:, h], ag[:, h], zt[:, h], ALU.add))
                        own.do(V.tensor_tensor(ag[:, h], ag[:, h], cols(dinv, n, h).unsqueeze(2).to_broadcast([P, J, D]),
                                               ALU.mult))
                        dve.wait_ge(s_st[h], 48 * n)
                        V.tensor_tensor(o_[:, h], ag[:, h], xs[:, h], ALU.add).then_inc(s_o[h], 1)
                        own.end()
                    batches(dve, step)


_INS = ['x', 'src', 'dst', 'edge_attr_32', 'edge_attr_96', 'edge_weight',
        'L0_gnn_Wq', 'L0_gnn_bq', 'L0_gnn_Wk', 'L0_gnn_bk', 'L0_gnn_We', 'L0_gnn_be', 'L0_gnn_Wv', 'L0_gnn_bv',
        'L1_gnn_mW1', 'L1_gnn_mb1', 'L1_gnn_mW2', 'L1_gnn_mb2', 'L1_gnn_gW1', 'L1_gnn_gb1', 'L1_gnn_gW2',
        'L1_gnn_gb2', 'L1_gnn_uW1', 'L1_gnn_ub1', 'L1_gnn_uW2', 'L1_gnn_ub2', 'L1_gnn_ln_g', 'L1_gnn_ln_b',
        'L3_gnn_W', 'L3_gnn_b']


def kernel(**inputs):
    import numpy as _np
    import concourse.bacc as _bacc
    from concourse import mybir as _mybir
    from concourse.bass_utils import run_bass_kernel_spmd as _run

    nc = _bacc.Bacc("TRN2", target_bir_lowering=False, num_devices=1)
    arrays, args = {}, []
    for name in _INS:
        a = _np.ascontiguousarray(inputs[name])
        arrays[f"in_{name}"] = a
        args.append(nc.dram_tensor(f"in_{name}", a.shape, _mybir.dt.from_np(a.dtype), kind="ExternalInput").ap())
    args.append(nc.dram_tensor("out_0", (N, D), F32, kind="ExternalOutput").ap())
    program(nc, *args)
    r = _run(nc, [arrays], core_ids=[0])
    return r.results[0]["out_0"]
```

```python
from contextlib import ExitStack

import concourse.bass as bass
from concourse import mybir

P = 128
N = 50000
D = 96
HEADS = 8
HD = D // HEADS
ED = 32
CH = -(-N // (P * 8)) * 8
J = 8
NB = CH // J
PAIRS = NB // 2
PER = [PAIRS + 1, PAIRS]
K = 4
OF = [len(range(h, NB, K)) for h in range(K)]
GB = K
ROWS = P * CH
FULL = P - 1
TAIL = N - FULL * CH
SPLIT = 112
AUX = ROWS
REG = ROWS + P
ZROW = REG
VALUES = ROWS
ROUNDS = 16
ALPHA = 0.1
NONE = 65535
WZ = D + HEADS
TR = D + 1
assert NB % 2 == 1 and 0 < TAIL < CH

F32 = mybir.dt.float32
I32 = mybir.dt.int32
ALU = mybir.AluOpType
ACT = mybir.ActivationFunctionType
AX = mybir.AxisListType.X
EPS = 1e-5


class Own:

    def __init__(self, eng, sem, per_step=0):
        self.eng, self.sem, self.per_step = eng, sem, per_step
        self.first, self.base, self.n = 0, 0, 0

    def loop(self):
        self.first, self.n = self.n, 0

    def step(self, index):
        self.base, self.n = index * self.per_step + self.first, 0

    def add(self, ins):
        ins.then_inc(self.sem, 1)
        self.n += 1

    def settle(self):
        self.eng.wait_ge(self.sem, self.base + self.n)

    def do(self, ins):
        self.add(ins)
        self.settle()

    def end(self):
        assert self.n == self.per_step, (self.n, self.per_step)


class Stream:

    def __init__(self, pair):
        self.pair, self.base = pair, [0] * K

    def __getitem__(self, h):
        return self.pair[h]

    def wait(self, eng, h, count):
        eng.wait_ge(self.pair[h], count + self.base[h])

    def close(self, of, passes=1):
        for h, batches_of in enumerate(of):
            self.base[h] += 16 * J * batches_of * passes


def after(eng, sem, count):
    if isinstance(count, int) and count < 1:
        return
    eng.wait_ge(sem, count)


def skewed(eng, *stages):
    def tick(q, u):
        for lag, run in stages:
            n, h = q + (u - lag) // K, (u - lag) % K
            if not isinstance(q, int) or 0 <= K * n + h < NB:
                run(K * n + h, n, h)

    lags = [lag for lag, _ in stages]
    first = 1 - (-max(lags)) // K
    last = (NB - 1 + min(min(lags), 0)) // K
    for t in range(min(lags), first * K):
        tick(t // K, t % K)
    with eng.Fori(first, last) as q:
        for u in range(K):
            tick(q, u)
    for t in range(last * K, NB + max(lags)):
        tick(t // K, t % K)


def batches(eng, step):
    step(0, 0)
    step(0, 1)
    with eng.Fori(1, PAIRS) as i:
        step(i, 0)
        step(i, 1)
    step(PAIRS, 0)


def ahead(eng, early, late):
    early(0, 0)
    early(0, 1)
    late(0, 0)
    early(1, 0)
    late(0, 1)
    with eng.Fori(1, PAIRS) as i:
        early(i, 1)
        late(i, 0)
        early(i + 1, 0)
        late(i, 1)
    late(PAIRS, 0)


def program(nc, x, src, dst, edge_attr_32, edge_attr_96, edge_weight,
            Wq, bq, Wk, bk, We, be, Wv, bv,
            mW1, mb1, mW2, mb2, gW1, gb1, gW2, gb2, uW1, ub1, uW2, ub2, ln_g, ln_b, W3, b3, out):
    V, A, T, G = nc.vector, nc.scalar, nc.tensor, nc.gpsimd
    outer = ExitStack()

    def dram(name, rows, width):
        return nc.dram_tensor(name, [rows, width], F32, kind="Internal").ap()

    kv_t = dram("kv_t", ROWS, 2 * D)
    q_t = dram("q_t", ROWS, D)
    info_t = dram("info_t", ROWS, 4)
    agg0_t = dram("agg0_t", REG + 1, WZ)
    agg1_t = dram("agg1_t", REG + 1, D)
    agg3_t = dram("agg3_t", REG + 1, D)
    x1_t = dram("x1_t", ROWS, D)
    x2_t = dram("x2_t", ROWS, D)
    x3_t = dram("x3_t", ROWS, D)
    rec_t = dram("rec_t", ROWS, TR)
    y_t = [dram(f"y{k}_t", VALUES + REG, D) for k in range(2)]
    c_t = dram("c_t", ROWS, D)
    z_t = dram("z_t", ROWS, D)
    x_tail = dram("x_tail", CH, D)
    e96_tail = dram("e96_tail", CH, D)
    e32_tail = dram("e32_tail", CH, ED)
    out_tail = dram("out_tail", CH, D)

    with outer:
        def sb(name, shape, dt=F32, ctx=outer):
            return ctx.enter_context(nc.sbuf_tensor(name, shape, dt))

        def ps(name, shape, ctx):
            return ctx.enter_context(nc.psum_tensor(name, shape, F32))

        s_stream = [Stream([nc.alloc_semaphore(name=f"gathered{k}_{h}") for h in range(K)]) for k in range(3)]
        s_single = nc.alloc_semaphore(name="gathered_single")
        of_pass = []

        def sem(name):
            of_pass.append(nc.alloc_semaphore(name=name))
            return of_pass[-1]

        def retire():
            with nc.Block() as block:
                @block.sync
                def _(sp):
                    for s in of_pass:
                        sp.sem_clear(s)
            for s in of_pass:
                nc.release_semaphore(s)
            of_pass.clear()

        def sems(name):
            return [sem(f"{name}_{h}") for h in range(2)]

        def quad(name):
            return [sem(f"{name}_{h}") for h in range(K)]

        def cols(t, b):
            return t[:, bass.ds(b * J, J)]

        def rows_of(table, first, b):
            return table[first:first + ROWS, :].rearrange("(p j) d -> p j d", p=P)[:, bass.ds(b * J, J), :]

        def load_padded(eng, tile, whole, tail, b, done):
            v = whole[0:FULL * CH, :].rearrange("(p j) d -> p j d", j=CH)
            c = bass.ds(b * J, J)
            eng.dma_start(tile[0:SPLIT], v[0:SPLIT, c, :]).then_inc(done, 16)
            eng.dma_start(tile[SPLIT:FULL], v[SPLIT:FULL, c, :]).then_inc(done, 16)
            eng.dma_start(tile[FULL:P], tail.rearrange("(a j) d -> a j d", a=1)[:, c, :]).then_inc(done, 16)

        def load_column(eng, tile, vec, first, done):
            v = vec[first:first + FULL * CH].rearrange("(p j) -> p j", j=CH)
            rest = vec[first + FULL * CH:N].rearrange("(a j) -> a j", a=1)
            eng.dma_start(tile[0:SPLIT], v[0:SPLIT]).then_inc(done, 16)
            eng.dma_start(tile[SPLIT:FULL], v[SPLIT:FULL]).then_inc(done, 16)
            eng.dma_start(tile[FULL:P, 0:N - first - FULL * CH], rest).then_inc(done, 16)

        ident = sb("ident", [P, P])
        B = sb("B", [P, P])
        src_i = sb("src_i", [P, CH], I32)
        dst_i = sb("dst_i", [P, CH], I32)
        scan = sb("scan", [P, CH, 3])
        k_e = sb("k_e", [P, CH])
        k_z = sb("k_z", [P, 1])
        ptr_n = sb("ptr_n", [P, CH])
        ptr_i = sb("ptr_i", [P, CH], I32)
        yptr_i = sb("yptr_i", [P, CH], I32)
        root = sb("root", [P, CH])
        iroot = sb("iroot", [P, CH])
        dinv = sb("dinv", [P, CH])
        ptr_e = sb("ptr_e", [P, CH])
        eps = sb("eps", [P, 1])
        zeros = sb("zeros", [P, WZ])
        scan_s = sb("scan_s", [P, K, J, 3])
        idx_s = sb("idx_s", [P, K, J], I32)
        F = sb("F", [P, WZ])
        Z = sb("Z", [P, WZ])
        s_turn_v, s_turn_p, s_turn_s = (nc.alloc_semaphore(name=f"{e}_turns") for e in ("vector", "pool", "sync"))
        s_w = sem("weights_loaded")
        weight_loads = []

        def weight(name, parts, width, rows=D + 1):
            t = sb(name, [rows, width])
            for r0, r1, c0, c1, a in parts:
                weight_loads.append((t[r0:r1, c0:c1], a))
            return t

        def row(v):
            return v.rearrange("(a n) -> a n", a=1)

        def col(v):
            return v.rearrange("(n a) -> n a", a=1)

        w_kvq = weight("w_kvq", [(0, D, 0, D, Wk), (0, D, D, 2 * D, Wv), (0, D, 2 * D, 3 * D, Wq),
                                 (D, D + 1, 0, D, row(bk)), (D, D + 1, D, 2 * D, row(bv)),
                                 (D, D + 1, 2 * D, 3 * D, row(bq))], 3 * D)
        w_e = weight("w_e", [(0, D, 0, D, We), (D, D + 1, 0, D, row(be))], D)
        w_m1 = weight("w_m1", [(0, ED, 0, D, mW1[D:D + ED, :]), (ED, P, 0, D, mW1[0:D, :])], D, P)
        w_g1 = weight("w_g1", [(0, ED, 0, D, gW1[D:D + ED, :]), (ED, P, 0, D, gW1[0:D, :])], D, P)
        w_m2 = weight("w_m2", [(0, D, 0, D, mW2), (D, D + 1, 0, D, row(mb2))], D)
        w_g2 = weight("w_g2", [(0, D, 0, 1, gW2), (D, D + 1, 0, 1, row(gb2))], 1)
        w_ua = weight("w_ua", [(0, D, 0, D, uW1[0:D, :])], D, D)
        w_ub = weight("w_ub", [(0, D, 0, D, uW1[D:2 * D, :])], D, D)
        w_u2 = weight("w_u2", [(0, D, 0, D, uW2), (D, D + 1, 0, D, row(ub2))], D)
        w_3 = weight("w_3", [(0, D, 0, D, W3)], D, D)
        c_m1 = weight("c_m1", [(0, D, 0, 1, col(mb1))], 1, D)
        c_g1 = weight("c_g1", [(0, D, 0, 1, col(gb1))], 1, D)
        c_u1 = weight("c_u1", [(0, D, 0, 1, col(ub1))], 1, D)
        r_rows = weight("r_rows", [(0, 1, 0, D, row(ln_g)), (0, 1, D, 2 * D, row(ln_b)),
                                   (0, 1, 2 * D, 3 * D, row(b3))], 3 * D, 1)
        r_all = sb("r_all", [P, 3, D])

        def ln_stats(dve, own, b, xin, st, mv, s_mv):
            own.step(b)
            for j in range(J):
                last = V.bn_stats(st[:, j, :], xin[:, j, :])
            own.do(last)
            own.end()
            dve.sem_inc(s_turn_v)
            for j in range(J):
                last = V.bn_aggr(mv[:, j, :], st[:, j, :])
            last.then_inc(s_mv, 1)

        def ln_root(act, b, mv, rn, s_mv, s_sd):
            after(act, s_mv, b + 1)
            A.activation(rn[:, 2, :], mv[:, :, 1], ACT.Sqrt, bias=eps[:]).then_inc(s_sd, 1)

        def ln_scale(dve, own, b, mv, rn, s_sd, s_rn):
            after(dve, s_sd, b + 1)
            own.do(V.reciprocal(rn[:, 0, :], rn[:, 2, :]))
            V.scalar_tensor_tensor(out=rn[:, 1, :], in0=mv[:, :, 0], scalar=-1.0, in1=rn[:, 0, :],
                                   op0=ALU.mult, op1=ALU.mult).then_inc(s_rn, 1)

        def ln_norm(act, b, xin, to, rn, s_rn, func):
            after(act, s_rn, b + 1)
            for j in range(J):
                last = A.activation(to[:, j, :], xin[:, j, :], func, scale=rn[:, 0, j:j + 1], bias=rn[:, 1, j:j + 1])
            return last

        def gather_slots(act, n, h, index, s_idx, s_free, per):
            s_free.wait(act, h, per * n)
            A.copy(idx_s[:, h, :], cols(index, 2 * n + h)).then_inc(s_idx[h], 1)

        def gathers(table, to, h, done):
            G.sem_inc(s_turn_p)
            for j in range(J):
                G.indirect_dma_start(out=to(j), out_offset=None, in_=table,
                                     in_offset=bass.IndirectOffsetOnAxis(ap=idx_s[:, h, j:j + 1], axis=0)
                                     ).then_inc(done, 16)

        def scan_step(dve, own, h, w, g, S, slots=2, s_s=None, done=None):
            for j in range(J):
                before = S[:, (h - 1) % slots, J - 1, 0:w] if j == 0 else S[:, h % slots, j - 1, 0:w]
                own.add(V.scalar_tensor_tensor(out=S[:, h % slots, j, 0:w], in0=before, scalar=scan_s[:, h, j, 0:1],
                                               in1=g[:, j, 0:w], op0=ALU.mult, op1=ALU.add))
                last = V.scalar_tensor_tensor(out=F[:, 0:w], in0=g[:, j, 0:w], scalar=scan_s[:, h, j, 1:2],
                                              in1=F[:, 0:w], op0=ALU.mult, op1=ALU.add)
                if j < J - 1 or s_s is None:
                    own.add(last)
                else:
                    last.then_inc(s_s, 1)
                own.settle()
            if s_s is not None:
                dve.wait_ge(s_s, done)

        def pointers(own, ptr, no, start, t, to, base):
            own.do(V.scalar_tensor_tensor(out=t, in0=ptr[:], scalar=-1.0, in1=start[:], op0=ALU.mult, op1=ALU.add))
            own.do(V.tensor_scalar(t, t, -float(base), None, ALU.add))
            own.do(V.tensor_tensor(t, t, no[:], ALU.mult))
            own.do(V.scalar_tensor_tensor(out=t, in0=ptr[:], scalar=float(base), in1=t, op0=ALU.add, op1=ALU.add))
            own.add(V.tensor_copy(to[:], t))

        with ExitStack() as ph:
            nxt_i = sb("nxt_i", [P, CH], I32, ph)
            dst_f = sb("dst_f", [P, CH], F32, ph)
            nxt_f = sb("nxt_f", [P, CH], F32, ph)
            wts = sb("wts", [P, CH], F32, ph)
            m = sb("m", [P, CH], F32, ph)
            fm = sb("fm", [P, CH], F32, ph)
            ones = sb("ones", [P, CH], F32, ph)
            cnt = sb("cnt", [P, CH], F32, ph)
            wsum = sb("wsum", [P, CH], F32, ph)
            row_i = sb("row_i", [P, CH], I32, ph)
            row_f = sb("row_f", [P, CH], F32, ph)
            aux_i = sb("aux_i", [P, 1], I32, ph)
            aux_f = sb("aux_f", [P, 1], F32, ph)
            tmp = sb("tmp", [P, CH], F32, ph)
            diag = sb("diag", [P, P], F32, ph)
            tri = sb("tri", [P, P], F32, ph)
            ends = sb("ends", [P, 2], F32, ph)
            carry = sb("carry", [P, 2], F32, ph)
            cz = sb("cz", [P, 1], F32, ph)
            seg = sb("seg", [P, CH, 4], F32, ph)
            seg_i = sb("seg_i", [P, CH], I32, ph)
            none = sb("none", [P, CH, 4], F32, ph)
            p_first = ps("p_first", [P, P], ph)
            p_carry = ps("p_carry", [P, 2], ph)
            s_pad, s_in, s_tail, s_init = sem("padding_set"), sem("edges_loaded"), sem("tails_written"), sem("info_set")
            s_iota, s_zero, s_v, s_diag, s_pf = (sem("iotas"), sem("zeros_set"), sem("graph_vector"),
                                                 sem("diag_ready"), sem("first_broadcast"))
            s_b, s_pc, s_bc = sem("b_and_ends"), sem("carry_summed"), sem("rows_broadcast")
            s_none = sem("none_ready")

            with nc.Block() as block:
                @block.sync
                def _(sp):
                    sp.wait_ge(s_pad, 4)
                    load_column(sp, dst_i, dst, 0, s_in)
                    load_column(sp, nxt_i, dst, 1, s_in)
                    load_column(sp, src_i, src, 0, s_in)
                    load_column(sp, wts, edge_weight, 0, s_in)
                    for to, a in weight_loads:
                        sp.dma_start(to, a).then_inc(s_w, 16)
                    sp.wait_ge(s_zero, 1)
                    for tail, whole, w in ((x_tail, x, D), (e96_tail, edge_attr_96, D), (e32_tail, edge_attr_32, ED)):
                        sp.dma_start(tail[0:TAIL, :], whole[FULL * CH:N, :]).then_inc(s_tail, 16)
                        sp.dma_start(tail[TAIL:TAIL + 96, :], zeros[0:96, 0:w]).then_inc(s_tail, 16)
                        sp.dma_start(tail[TAIL + 96:CH, :], zeros[0:CH - TAIL - 96, 0:w]).then_inc(s_tail, 16)
                    for t in (agg0_t, agg1_t, agg3_t):
                        sp.dma_start(t[ZROW:ZROW + 1, :], zeros[0:1, 0:t.shape[1]]).then_inc(s_tail, 16)
                    sp.wait_ge(s_none, 2)
                    sp.dma_start(info_t.rearrange("(p j) d -> p j d", p=P), none[:]).then_inc(s_init, 16)
                    sp.wait_ge(s_tail, 16 * 12)
                    sp.wait_ge(s_init, 16)
                    sp.wait_ge(s_w, 16 * len(weight_loads))

                @block.gpsimd
                def _(pool):
                    G.memset(ident[:], 0.0).then_inc(s_iota, 1)
                    pool.wait_ge(s_iota, 1)
                    G.affine_select(out=ident[:], in_=ident[:], compare_op=ALU.not_equal, fill=1.0, base=0,
                                    pattern=[[-1, P]], channel_multiplier=1).then_inc(s_iota, 1)
                    G.memset(tri[:], 1.0).then_inc(s_iota, 1)
                    pool.wait_ge(s_iota, 3)
                    G.affine_select(out=tri[:], in_=tri[:], compare_op=ALU.is_gt, fill=0.0, base=0,
                                    pattern=[[1, P]], channel_multiplier=-1).then_inc(s_iota, 1)
                    G.iota(row_i[:], [[1, CH]], base=0, channel_multiplier=CH).then_inc(s_iota, 1)
                    G.iota(aux_i[:], [[1, 1]], base=AUX, channel_multiplier=1).then_inc(s_iota, 1)
                    pool.wait_ge(s_w, 16 * len(weight_loads))
                    G.partition_broadcast(r_all[:].rearrange("p a d -> p (a d)"), r_rows[:]).then_inc(s_bc, 1)

                @block.tensor
                def _(pe):
                    pe.wait_ge(s_diag, 1)
                    T.matmul(p_first[:], ones[:, 0:P], diag[:], start=True, stop=True).then_inc(s_pf, 1)
                    pe.wait_ge(s_b, 1)
                    T.matmul(p_carry[:], B[:], ends[:], start=True, stop=True).then_inc(s_pc, 1)

                @block.vector
                def _(dve):
                    own = Own(dve, s_v)
                    V.memset(dst_i[:], NONE).then_inc(s_pad, 1)
                    V.memset(nxt_i[:], NONE).then_inc(s_pad, 1)
                    V.memset(src_i[:], 0).then_inc(s_pad, 1)
                    V.memset(wts[:], 0.0).then_inc(s_pad, 1)
                    V.memset(zeros[:], 0.0).then_inc(s_zero, 1)
                    own.add(V.memset(ones[:], 1.0))
                    own.add(V.memset(eps[:], EPS))
                    own.do(V.memset(none[:], 0.0))
                    V.memset(none[:, :, 0:1], float(ZROW)).then_inc(s_none, 2)
                    own.add(V.memset(m[:, 0:1], 0.0))
                    own.add(V.memset(seg[:], 0.0))
                    dve.wait_ge(s_in, 16 * 12)
                    dve.wait_ge(s_iota, 6)
                    own.add(V.tensor_copy(dst_f[:], dst_i[:]))
                    own.add(V.tensor_copy(nxt_f[:], nxt_i[:]))
                    own.add(V.tensor_copy(row_f[:], row_i[:]))
                    own.do(V.tensor_copy(aux_f[:], aux_i[:]))
                    own.settle()
                    V.tensor_scalar(diag[:], ident[:], dst_f[:, 0:1], None, ALU.mult).then_inc(s_diag, 1)
                    own.add(V.tensor_tensor(m[:, 1:CH], dst_f[:, 1:CH], dst_f[:, 0:CH - 1], ALU.is_equal))
                    own.do(V.tensor_scalar(fm[:], dst_f[:], dst_f[:, 0:1], None, ALU.is_equal))
                    own.add(V.tensor_tensor_scan(cnt[:], m[:], ones[:], 0.0, ALU.mult, ALU.add))
                    own.do(V.tensor_tensor_scan(wsum[:], m[:], wts[:], 0.0, ALU.mult, ALU.add))
                    own.add(V.tensor_copy(ends[:, 0:1], cnt[:, CH - 1:CH]))
                    own.add(V.tensor_copy(ends[:, 1:2], wsum[:, CH - 1:CH]))
                    dve.wait_ge(s_pf, 1)
                    own.do(V.tensor_scalar(B[:], p_first[:], dst_f[:, CH - 1:CH], None, ALU.is_equal))
                    V.tensor_tensor(B[:], B[:], tri[:], ALU.mult).then_inc(s_b, 1)
                    dve.wait_ge(s_pc, 1)
                    own.do(V.tensor_copy(carry[:], p_carry[:]))
                    own.add(V.scalar_tensor_tensor(out=cnt[:], in0=fm[:], scalar=carry[:, 0:1], in1=cnt[:],
                                                   op0=ALU.mult, op1=ALU.add))
                    own.add(V.scalar_tensor_tensor(out=wsum[:], in0=fm[:], scalar=carry[:, 1:2], in1=wsum[:],
                                                   op0=ALU.mult, op1=ALU.add))
                    own.do(V.reduce_sum(cz[:], fm[:], AX))
                    own.do(V.tensor_tensor(cz[:], cz[:], carry[:, 0:1], ALU.add))
                    own.add(V.tensor_scalar(cz[:], cz[:], 1.0, None, ALU.add))
                    own.do(V.tensor_scalar(tmp[:], cnt[:], 1.0, None, ALU.add))
                    own.add(V.reciprocal(k_e[:], tmp[:]))
                    own.do(V.reciprocal(k_z[:], cz[:]))
                    own.add(V.tensor_scalar(k_e[:], k_e[:], 1.0 - ALPHA, None, ALU.mult))
                    own.add(V.tensor_scalar(k_z[:], k_z[:], 1.0 - ALPHA, None, ALU.mult))
                    own.do(V.tensor_scalar(tmp[:], row_f[:], -1.0, aux_f[:], ALU.mult, ALU.add))
                    own.do(V.tensor_tensor(tmp[:], tmp[:], fm[:], ALU.mult))
                    own.add(V.tensor_tensor(seg[:, :, 0], tmp[:], row_f[:], ALU.add))
                    own.add(V.tensor_copy(seg[:, :, 1], cnt[:]))
                    own.add(V.tensor_copy(seg[:, :, 2], wsum[:]))
                    own.do(V.tensor_tensor(nxt_f[:], dst_f[:], nxt_f[:], ALU.is_equal))
                    own.do(V.scalar_tensor_tensor(out=tmp[:], in0=nxt_f[:], scalar=float(2 * NONE), in1=dst_f[:],
                                                  op0=ALU.mult, op1=ALU.add))
                    own.add(V.tensor_copy(seg_i[:], tmp[:]))
                    own.add(V.tensor_copy(scan[:, :, 0], m[:]))
                    own.add(V.tensor_copy(scan[:, :, 1], fm[:]))
                    own.do(V.tensor_copy(scan[:, :, 2], wts[:]))
                    own.do(V.tensor_scalar(tmp[:], dst_f[:], float(N), None, ALU.is_lt))
                    own.do(V.tensor_tensor(tmp[:], tmp[:], dst_f[:], ALU.mult))
                    own.do(V.tensor_copy(dst_i[:], tmp[:]))

            with ExitStack() as p0:
                xs = sb("n0_x", [P, K, J, D], F32, p0)
                hh = sb("n0_h", [P, K, J, D], F32, p0)
                hT = sb("n0_hT", [D + 1, K, 2, 4 * P], F32, p0)
                kvq = sb("n0_kvq", [P, K, J, 3 * D], F32, p0)
                st = sb("n0_st", [P, K, J, 6], F32, p0)
                mv = sb("n0_mv", [P, K, J, 2], F32, p0)
                rn = sb("n0_rn", [P, K, 3, J], F32, p0)
                seg_s = sb("seg_s", [P, K, J, 4], F32, p0)
                tp = [ps(f"n0_tp{g}", [P, 4 * P], p0) for g in range(2)]
                ob = [ps(f"n0_ob{k}", [P, 3 * D], p0) for k in range(4)]
                s_x, s_st, s_sc = quad("n0_x_in"), quad("n0_stored"), s_stream[0]
                s_mv, s_sd, s_rn, s_h, s_tp, s_tc, s_om, s_ocd, s_oca, s_sl, s_one = map(sem, (
                    "n0_stats", "n0_root", "n0_scale", "n0_h_ready", "n0_tp_full", "n0_tp_copied", "n0_ob_full",
                    "n0_even_copied", "n0_odd_copied", "n0_slots", "n0_ones"))
                s_own1, s_own2 = sem("n0_vector_stats"), sem("n0_vector_scale")

                with nc.Block() as block:
                    @block.sync
                    def _(sp):
                        def load(b, n, h):
                            after(sp, s_h, b - 3)
                            load_padded(sp, xs[:, h], x, x_tail, b, s_x[h])

                        def store(b, n, h):
                            after(sp, s_ocd, 4 * b + 4)
                            after(sp, s_oca, 4 * b + 4)
                            sp.dma_start(rows_of(kv_t, 0, b), kvq[:, h, :, 0:2 * D]).then_inc(s_st[h], 16)
                            sp.dma_start(rows_of(q_t, 0, b), kvq[:, h, :, 2 * D:3 * D]).then_inc(s_st[h], 16)
                        skewed(sp, (-2, load), (3, store))
                        for h in range(K):
                            sp.wait_ge(s_st[h], 32 * OF[h])

                    @block.gpsimd
                    def _(pool):
                        bound = pool.to_reg(ROWS - 1)
                        G.memset(hT[D:D + 1], 1.0).then_inc(s_one, 1)

                        def step(b, n, h):
                            after(pool, s_sl, 2 * b + 2)
                            pool.sem_inc(s_turn_p)
                            for j in range(J):
                                G.indirect_dma_start(
                                    out=info_t, out_offset=bass.IndirectOffsetOnAxis(ap=idx_s[:, h, j:j + 1], axis=0),
                                    in_=seg_s[:, h, j, :], in_offset=None, bounds_check=bound, oob_is_err=False
                                ).then_inc(s_sc[h], 16)
                        skewed(pool, (0, step))
                        for h in range(K):
                            s_sc.wait(pool, h, 16 * J * OF[h])

                    @block.vector
                    def _(dve):
                        own1, own2 = Own(dve, s_own1, 1), Own(dve, s_own2, 1)

                        def slots(b, n, h):
                            s_sc.wait(dve, h, 16 * J * n)
                            V.tensor_copy(idx_s[:, h, :], cols(seg_i, b)).then_inc(s_sl, 1)
                            V.tensor_copy(seg_s[:, h], cols(seg, b)).then_inc(s_sl, 1)

                        def scale(b, n, h):
                            after(dve, s_h, b - 3)
                            own2.step(b)
                            ln_scale(dve, own2, b, mv[:, h], rn[:, h], s_sd, s_rn)

                        def copy(b, n, h):
                            dve.wait_ge(s_st[h], 32 * n)
                            for j in range(0, J, 2):
                                after(dve, s_om, 8 * b + j + 1)
                                V.tensor_copy(kvq[:, h, j, :], ob[j % 4][:]).then_inc(s_ocd, 1)

                        def stats(b, n, h):
                            dve.wait_ge(s_x[h], 48 * (n + 1))
                            after(dve, s_rn, b - 3)
                            ln_stats(dve, own1, b, xs[:, h], st[:, h], mv[:, h], s_mv)
                        skewed(dve, (0, slots), (1, scale), (3, copy), (0, stats))

                    @block.scalar
                    def _(act):
                        def norm(b, n, h):
                            after(act, s_tp, 2 * b - 6)
                            ln_norm(act, b, xs[:, h], hh[:, h], rn[:, h], s_rn, ACT.Relu).then_inc(s_h, 1)

                        def copy(b, n, h):
                            act.wait_ge(s_st[h], 32 * n)
                            for j in range(1, J, 2):
                                after(act, s_om, 8 * b + j + 1)
                                A.copy(kvq[:, h, j, :], ob[j % 4][:]).then_inc(s_oca, 1)

                        def turned(b, n, h):
                            after(act, s_om, 8 * b - 24)
                            for g in range(2):
                                after(act, s_tp, 2 * b + g + 1)
                                A.copy(hT[0:D, h, g, :], tp[g][0:D, :]).then_inc(s_tc, 1)
                        skewed(act, (1, norm), (3, copy), (2, turned), (0, lambda b, n, h: ln_root(
                            act, b, mv[:, h], rn[:, h], s_mv, s_sd)))

                    @block.tensor
                    def _(pe):
                        pe.wait_ge(s_one, 1)

                        def turn(b, n, h):
                            after(pe, s_h, b + 1)
                            for g in range(2):
                                after(pe, s_tc, 2 * b + g - 1)
                                for j in range(4):
                                    last = T.transpose(tp[g][0:D, j * P:(j + 1) * P], hh[:, h, 4 * g + j, :], ident[:])
                                last.then_inc(s_tp, 1)

                        def product(b, n, h):
                            for j in range(J):
                                if j % 4 == 0:
                                    after(pe, s_tc, 2 * b + j // 4 + 1)
                                after(pe, s_oca if j % 2 else s_ocd, 4 * b + j // 2 - 1)
                                T.matmul(ob[j % 4][:], hT[:, h, j // 4, j % 4 * P:(j % 4 + 1) * P], w_kvq[:],
                                         start=True, stop=True).then_inc(s_om, 1)
                        skewed(pe, (3, product), (2, turn))

        s_sc.close(OF)
        retire()

        with ExitStack() as ph:
            info = sb("info", [P, CH, 4], F32, ph)
            no = sb("no", [P, CH], F32, ph)
            node_i = sb("node_i", [P, CH], I32, ph)
            node_f = sb("node_f", [P, CH], F32, ph)
            t0 = sb("t0", [P, CH], F32, ph)
            t1 = sb("t1", [P, CH], F32, ph)
            s_in, s_it, s_v, s_r, s_q = (sem("info_loaded"), sem("node_iota"), sem("info_vector"), sem("degrees_ready"),
                                         sem("degree_roots"))
            with nc.Block() as block:
                @block.sync
                def _(sp):
                    sp.dma_start(info[:], info_t.rearrange("(p j) d -> p j d", p=P)).then_inc(s_in, 16)

                @block.gpsimd
                def _(pool):
                    G.iota(node_i[:], [[1, CH]], base=0, channel_multiplier=CH).then_inc(s_it, 1)

                @block.scalar
                def _(act):
                    act.wait_ge(s_r, 2)
                    A.activation(root[:], t0[:], ACT.Sqrt).then_inc(s_q, 1)
                    A.activation(t1[:], t1[:], ACT.Sqrt).then_inc(s_q, 1)

                @block.vector
                def _(dve):
                    own = Own(dve, s_v)
                    dve.wait_ge(s_in, 16)
                    dve.wait_ge(s_it, 1)
                    V.tensor_scalar(t0[:], info[:, :, 1], 1.0, None, ALU.add).then_inc(s_r, 1)
                    own.add(V.tensor_copy(ptr_n[:], info[:, :, 0]))
                    own.add(V.tensor_copy(node_f[:], node_i[:]))
                    own.do(V.tensor_scalar(dinv[:], info[:, :, 2], 1.0, None, ALU.add))
                    V.tensor_scalar(t1[:], dinv[:], 1e-30, None, ALU.max).then_inc(s_r, 1)
                    own.add(V.tensor_copy(ptr_i[:], ptr_n[:]))
                    own.do(V.tensor_scalar(no[:], ptr_n[:], float(ZROW), None, ALU.is_equal))
                    pointers(own, ptr_n, no, node_f, info[:, :, 3], yptr_i, VALUES)
                    dve.wait_ge(s_q, 2)
                    own.add(V.reciprocal(iroot[:], root[:]))
                    own.add(V.reciprocal(t1[:], t1[:]))
                    own.do(V.tensor_scalar(dinv[:], dinv[:], 0.0, None, ALU.is_gt))
                    own.do(V.tensor_tensor(dinv[:], dinv[:], t1[:], ALU.mult))
        retire()

        with ExitStack() as p1:
            gkv = sb("e0_kv", [P, 2, J, 2 * D], F32, p1)
            gq = sb("e0_q", [P, 2, J, D], F32, p1)
            ea = sb("e0_ea", [P, 2, J, D], F32, p1)
            eaT = sb("e0_eaT", [D + 1, 2, 2, 4 * P], F32, p1)
            dst_s = sb("dst_s", [P, 2, J], I32, p1)
            g_ = sb("e0_g", [P, 2, J, WZ], F32, p1)
            S = sb("e0_S", [P, 2, J, WZ], F32, p1)
            sc = sb("e0_sc", [P, 2, J, HEADS], F32, p1)
            tp = [ps(f"e0_tp{g}", [P, 4 * P], p1) for g in range(2)]
            eo = [ps(f"e0_eo{g}", [P, 4, D], p1) for g in range(2)]
            pc = ps("e0_pc", [P, WZ], p1)
            s_ei, s_ix, s_gk, s_gq, s_rd, s_sc, s_ex, s_s, s_st = (
                sems("e0_ea_in"), sems("e0_rows_set"), s_stream[0], s_stream[1],
                sems("e0_msg_done"), sems("e0_scores"), sems("e0_exp"), sems("e0_sums"), sems("e0_stored"))
            s_tp = [sems(f"e0_tp{g}_full") for g in range(2)]
            s_tc = [sems(f"e0_tp{g}_copied") for g in range(2)]
            s_eo = [sems(f"e0_eo{g}_full") for g in range(2)]
            s_eu = [sems(f"e0_eo{g}_used") for g in range(2)]
            s_own, s_one, s_cr, s_z, s_zo = (sem("e0_vector"), sem("e0_ones"), sem("e0_carry"), sem("e0_first_sums"),
                                             sem("e0_first_stored"))

            with nc.Block() as block:
                @block.sync
                def _(sp):
                    def load(n, h):
                        sp.wait_ge(s_tp[1][h], n)
                        load_padded(sp, ea[:, h], edge_attr_96, e96_tail, 2 * n + h, s_ei[h])

                    def store(n, h):
                        sp.wait_ge(s_s[h], n + 1)
                        sp.dma_start(rows_of(agg0_t, 0, 2 * n + h), S[:, h]).then_inc(s_st[h], 16)
                    ahead(sp, load, store)
                    sp.wait_ge(s_z, 1)
                    sp.dma_start(agg0_t[AUX:AUX + P, :], Z[:]).then_inc(s_zo, 16)
                    sp.wait_ge(s_st[0], 16 * (PAIRS + 1))
                    sp.wait_ge(s_st[1], 16 * PAIRS)
                    sp.wait_ge(s_zo, 16)

                @block.gpsimd
                def _(pool):
                    G.memset(eaT[D:D + 1], 1.0).then_inc(s_one, 1)

                    def step(n, h):
                        pool.wait_ge(s_ix[h], 3 * n + 3)
                        pool.wait_ge(s_rd[h], n)
                        gathers(kv_t, lambda j: gkv[:, h, j, :], h, s_gk[h])
                        for j in range(J):
                            G.indirect_dma_start(out=gq[:, h, j, :], out_offset=None, in_=q_t,
                                                 in_offset=bass.IndirectOffsetOnAxis(ap=dst_s[:, h, j:j + 1], axis=0)
                                                 ).then_inc(s_gq[h], 16)
                    batches(pool, step)

                @block.tensor
                def _(pe):
                    pe.wait_ge(s_one, 1)

                    def step(n, h):
                        pe.wait_ge(s_ei[h], 48 * (n + 1))
                        for g in range(2):
                            pe.wait_ge(s_tc[g][1 - h], n + h)
                            for j in range(4):
                                last = T.transpose(tp[g][0:D, j * P:(j + 1) * P], ea[:, h, 4 * g + j, :], ident[:])
                            last.then_inc(s_tp[g][h], 1)
                        for g in range(2):
                            pe.wait_ge(s_tc[g][h], n + 1)
                            pe.wait_ge(s_eu[g][1 - h], n + h)
                            for j in range(4):
                                last = T.matmul(eo[g][:, j, :], eaT[:, h, g, j * P:(j + 1) * P], w_e[:],
                                                start=True, stop=True)
                            last.then_inc(s_eo[g][h], 1)
                    batches(pe, step)
                    pe.wait_ge(s_s[0], PAIRS + 1)
                    T.matmul(pc[:], B[:], S[:, 0, J - 1, :], start=True, stop=True).then_inc(s_cr, 1)

                @block.scalar
                def _(act):
                    def early(n, h):
                        s_gk.wait(act, h, 16 * J * n)
                        s_gq.wait(act, h, 16 * J * n)
                        act.wait_ge(s_s[h], n)
                        A.copy(idx_s[:, h, :], cols(src_i, 2 * n + h)).then_inc(s_ix[h], 1)
                        A.copy(dst_s[:, h, :], cols(dst_i, 2 * n + h)).then_inc(s_ix[h], 1)
                        A.copy(scan_s[:, h], cols(scan, 2 * n + h)).then_inc(s_ix[h], 1)

                    def late(n, h):
                        for g in range(2):
                            act.wait_ge(s_tp[g][h], n + 1)
                            act.wait_ge(s_eo[1][h], n)
                            A.copy(eaT[0:D, h, g, :], tp[g][0:D, :]).then_inc(s_tc[g][h], 1)
                        act.wait_ge(s_sc[h], n + 1)
                        A.activation(g_[:, h, :, D:WZ], sc[:, h], ACT.Exp).then_inc(s_ex[h], 1)
                    ahead(act, early, late)

                @block.vector
                def _(dve):
                    own = Own(dve, s_own, 6 + 2 * J - 1)
                    own.add(V.memset(S[:], 0.0))
                    own.do(V.memset(F[:], 0.0))
                    own.loop()

                    def step(n, h):
                        own.step(2 * n + h)
                        s_gk.wait(dve, h, 16 * J * (n + 1))
                        s_gq.wait(dve, h, 16 * J * (n + 1))
                        own.do(V.tensor_tensor(gq[:, h], gq[:, h], gkv[:, h, :, 0:D], ALU.mult))
                        for g in range(2):
                            dve.wait_ge(s_eo[g][h], n + 1)
                            V.tensor_tensor(gq[:, h, 4 * g:4 * g + 4, :], gq[:, h, 4 * g:4 * g + 4, :], eo[g][:],
                                            ALU.mult).then_inc(s_eu[g][h], 1)
                        dve.wait_ge(s_eu[1][h], n + 1)
                        own.do(V.reduce_sum(sc[:, h].rearrange("p j a -> p (j a)"),
                                            gq[:, h].rearrange("p j (a d) -> p (j a) d", d=HD), AX))
                        own.do(V.tensor_scalar(sc[:, h], sc[:, h], HD ** -0.5, -5.0, ALU.mult, ALU.max))
                        V.tensor_scalar(sc[:, h], sc[:, h], 5.0, None, ALU.min).then_inc(s_sc[h], 1)
                        dve.wait_ge(s_ex[h], n + 1)
                        for j in range(0, J, 2):
                            last = V.tensor_tensor(
                                g_[:, h, j:j + 2, 0:D].rearrange("p j (a d) -> p j a d", d=HD),
                                gkv[:, h, j:j + 2, D:2 * D].rearrange("p j (a d) -> p j a d", d=HD),
                                g_[:, h, j:j + 2, D:WZ].unsqueeze(3).to_broadcast([P, 2, HEADS, HD]), ALU.mult)
                            own.add(last) if j < J - 2 else last.then_inc(s_rd[h], 1)
                        dve.wait_ge(s_rd[h], n + 1)
                        own.settle()
                        dve.wait_ge(s_st[h], 16 * n)
                        scan_step(dve, own, h, WZ, g_[:, h], S, 2, s_s[h], n + 1)
                        own.end()
                    batches(dve, step)
                    dve.wait_ge(s_cr, 1)
                    V.tensor_tensor(Z[:], F[:], pc[:], ALU.add).then_inc(s_z, 1)
        s_gk.close(PER)
        s_gq.close(PER)
        retire()

        with ExitStack() as p2:
            ag = sb("n1_ag", [P, K, J, WZ], F32, p2)
            xs = sb("n1_x", [P, K, J, D], F32, p2)
            xb = sb("n1_xb", [P, K, J, D], F32, p2)
            rz = sb("n1_rz", [P, K, J, HEADS], F32, p2)
            rec = sb("n1_rec", [P, K, J, TR], F32, p2)
            st = sb("n1_st", [P, K, J, 6], F32, p2)
            mv = sb("n1_mv", [P, K, J, 2], F32, p2)
            rn = sb("n1_rn", [P, K, 3, J], F32, p2)
            s_x, s_g, s_st = quad("n1_x_in"), s_stream[0], quad("n1_stored")
            s_ix, s_x1, s_xb, s_mv, s_sd, s_rn, s_pt, s_h, s_own0, s_own1, s_own2 = map(sem, (
                "n1_rows_set", "n1_x_updated", "n1_xb_ready", "n1_stats", "n1_root", "n1_scale", "n1_pointers_set",
                "n1_h_ready", "n1_vector_x", "n1_vector_stats", "n1_vector_scale"))
            with nc.Block() as block:
                @block.sync
                def _(sp):
                    def load(b, n, h):
                        after(sp, s_h, b - 3)
                        load_padded(sp, xs[:, h], x, x_tail, b, s_x[h])

                    def store(b, n, h):
                        after(sp, s_xb, b + 1)
                        sp.dma_start(rows_of(x1_t, 0, b), xb[:, h]).then_inc(s_st[h], 16)
                        after(sp, s_h, b + 1)
                        after(sp, s_pt, b + 1)
                        sp.dma_start(rows_of(rec_t, 0, b), rec[:, h]).then_inc(s_st[h], 16)
                    skewed(sp, (0, load), (2, store))
                    for h in range(K):
                        sp.wait_ge(s_st[h], 32 * OF[h])

                @block.gpsimd
                def _(pool):
                    def step(b, n, h):
                        after(pool, s_ix, b + 1)
                        after(pool, s_x1, b - 3)
                        gathers(agg0_t, lambda j: ag[:, h, j, :], h, s_g[h])
                    skewed(pool, (0, step))

                @block.vector
                def _(dve):
                    own0, own1, own2 = Own(dve, s_own0, 3), Own(dve, s_own1, 1), Own(dve, s_own2, 1)

                    def add(b, n, h):
                        own0.step(b)
                        s_g.wait(dve, h, 16 * J * (n + 1))
                        own0.do(V.tensor_scalar(rz[:, h], ag[:, h, :, D:WZ], 1e-6, None, ALU.add))
                        own0.do(V.reciprocal(rz[:, h], rz[:, h]))
                        for j in range(0, J, 2):
                            v = ag[:, h, j:j + 2, 0:D].rearrange("p j (a d) -> p j a d", d=HD)
                            last = V.tensor_tensor(v, v, rz[:, h, j:j + 2, :].unsqueeze(3).to_broadcast(
                                [P, 2, HEADS, HD]), ALU.mult)
                        own0.do(last)
                        own0.end()
                        dve.wait_ge(s_x[h], 48 * (n + 1))
                        V.tensor_tensor(xs[:, h], xs[:, h], ag[:, h, :, 0:D], ALU.add).then_inc(s_x1, 1)
                        after(dve, s_x1, b + 1)
                        after(dve, s_rn, b - 3)
                        ln_stats(dve, own1, b, xs[:, h], st[:, h], mv[:, h], s_mv)
                        dve.wait_ge(s_st[h], 32 * n)
                        V.tensor_tensor(xb[:, h], xs[:, h], r_all[:, 1:2, :].to_broadcast([P, J, D]), ALU.add
                                        ).then_inc(s_xb, 1)

                    def scale(b, n, h):
                        after(dve, s_h, b - 3)
                        own2.step(b)
                        ln_scale(dve, own2, b, mv[:, h], rn[:, h], s_sd, s_rn)
                    skewed(dve, (2, scale), (1, add))

                @block.scalar
                def _(act):
                    def slots(b, n, h):
                        s_g.wait(act, h, 16 * J * n)
                        A.copy(idx_s[:, h, :], cols(ptr_i, b)).then_inc(s_ix, 1)

                    def norm(b, n, h):
                        act.wait_ge(s_st[h], 32 * n)
                        A.copy(rec[:, h, :, D:TR], cols(ptr_n, b).unsqueeze(2)).then_inc(s_pt, 1)
                        after(act, s_xb, b + 1)
                        ln_norm(act, b, xs[:, h], rec[:, h, :, 0:D], rn[:, h], s_rn, ACT.Relu).then_inc(s_h, 1)
                    skewed(act, (-2, slots), (2, norm),
                           (1, lambda b, n, h: ln_root(act, b, mv[:, h], rn[:, h], s_mv, s_sd)))
        s_g.close(OF)
        retire()

        with ExitStack() as p3:
            xe = sb("e1_x", [P, K, J, ED + TR], F32, p3)
            xT = sb("e1_xT", [P, K, 2, 4 * P], F32, p3)
            mT = sb("e1_mT", [D + 1, K, 2, 4 * P], F32, p3)
            gT = sb("e1_gT", [D + 1, K, 2, 4 * P], F32, p3)
            gate = sb("e1_gate", [P, K, J, 1], F32, p3)
            g_ = sb("e1_g", [P, K, J, D], F32, p3)
            S = sb("e1_S", [P, K, J, D], F32, p3)
            tp = [ps(f"e1_tp{g}", [P, 4 * P], p3) for g in range(2)]
            pm = ps("e1_pm", [P, 4 * P], p3)
            pg = ps("e1_pg", [P, 4 * P], p3)
            po = [ps(f"e1_po{g}", [P, 4, D + 1], p3) for g in range(2)]
            pc = ps("e1_pc", [P, D], p3)
            s_e, s_g, s_st = quad("e1_ea_in"), s_stream[0], quad("e1_stored")
            s_ix, s_ms, s_pe, s_s, s_tp, s_tc, s_pm, s_pg, s_mt, s_gt, s_po, s_th, s_pu = map(sem, (
                "e1_rows_set", "e1_masks_set", "e1_pointers_kept", "e1_sums", "e1_tp_full", "e1_tp_copied", "e1_pm_full", "e1_pg_full",
                "e1_m_gelu", "e1_g_gelu", "e1_po_full", "e1_gate_tanh", "e1_po_used"))
            s_own1, s_own, s_one, s_cr, s_z, s_zo = map(sem, ("e1_vector_gates", "e1_vector_scan", "e1_ones", "e1_carry",
                                                              "e1_first_sums", "e1_first_stored"))
            with nc.Block() as block:
                @block.sync
                def _(sp):
                    def load(b, n, h):
                        after(sp, s_tp, 2 * b - 6)
                        load_padded(sp, xe[:, h, :, 0:ED], edge_attr_32, e32_tail, b, s_e[h])

                    def store(b, n, h):
                        after(sp, s_s, b + 1)
                        sp.dma_start(rows_of(agg1_t, 0, b), S[:, h]).then_inc(s_st[h], 16)
                    skewed(sp, (-1, load), (4, store))
                    sp.wait_ge(s_z, 1)
                    sp.dma_start(agg1_t[AUX:AUX + P, :], Z[:, 0:D]).then_inc(s_zo, 16)
                    for h in range(K):
                        sp.wait_ge(s_st[h], 16 * OF[h])
                    sp.wait_ge(s_zo, 16)

                @block.gpsimd
                def _(pool):
                    G.memset(mT[D:D + 1], 1.0).then_inc(s_one, 1)
                    G.memset(gT[D:D + 1], 1.0).then_inc(s_one, 1)

                    def step(b, n, h):
                        after(pool, s_ix, b + 1)
                        after(pool, s_tp, 2 * b - 6)
                        after(pool, s_pe, b - 3)
                        gathers(rec_t, lambda j: xe[:, h, j, ED:ED + TR], h, s_g[h])
                    skewed(pool, (0, step))

                @block.tensor
                def _(pe):
                    pe.wait_ge(s_one, 2)

                    def turn(b, n, h):
                        pe.wait_ge(s_e[h], 48 * (n + 1))
                        s_g.wait(pe, h, 16 * J * (n + 1))
                        for g in range(2):
                            after(pe, s_tc, 2 * b + g - 1)
                            for j in range(4):
                                last = T.transpose(tp[g][:, j * P:(j + 1) * P], xe[:, h, 4 * g + j, 0:P], ident[:])
                            last.then_inc(s_tp, 1)

                    def hidden(g):
                        def run(b, n, h):
                            after(pe, s_tc, 2 * b + g + 1)
                            for bank, w, full, used in ((pm, w_m1, s_pm, s_mt), (pg, w_g1, s_pg, s_gt)):
                                after(pe, used, 2 * b + g)
                                T.matmul(bank[0:D, :], w[:], xT[:, h, g, :], start=True, stop=True).then_inc(full, 1)
                        return run

                    def message(g):
                        def run(b, n, h):
                            after(pe, s_mt, 2 * b + 1 + g)
                            after(pe, s_gt, 2 * b + 1 + g)
                            after(pe, s_pu, 2 * b + g - 1)
                            for j in range(4):
                                c = slice(j * P, (j + 1) * P)
                                T.matmul(po[g][:, j, 0:D], mT[:, h, g, c], w_m2[:], start=True, stop=True)
                                last = T.matmul(po[g][:, j, D:D + 1], gT[:, h, g, c], w_g2[:], start=True, stop=True)
                            last.then_inc(s_po, 1)
                        return run
                    skewed(pe, (3, hidden(0)), (4, message(0)), (3, hidden(1)), (4, message(1)), (2, turn))
                    pe.wait_ge(s_s, NB)
                    T.matmul(pc[:], B[:], S[:, (NB - 1) % K, J - 1, :], start=True, stop=True).then_inc(s_cr, 1)

                @block.scalar
                def _(act):
                    def slots(b, n, h):
                        s_g.wait(act, h, 16 * J * n)
                        A.copy(idx_s[:, h, :], cols(src_i, b)).then_inc(s_ix, 1)

                    def masks(b, n, h):
                        after(act, s_s, b - 3)
                        A.copy(scan_s[:, h], cols(scan, b)).then_inc(s_ms, 1)

                    def keep(b, n, h):
                        s_g.wait(act, h, 16 * J * (n + 1))
                        A.copy(cols(ptr_e, b).unsqueeze(2), xe[:, h, :, ED + D:ED + TR]).then_inc(s_pe, 1)

                    def turned(b, n, h):
                        after(act, s_pg, 2 * b - 6)
                        for g in range(2):
                            after(act, s_tp, 2 * b + 1 + g)
                            A.copy(xT[:, h, g, :], tp[g][:]).then_inc(s_tc, 1)

                    def gelus(g):
                        def run(b, n, h):
                            after(act, s_po, 2 * b - 6)
                            after(act, s_pm, 2 * b + 1 + g)
                            A.activation(mT[0:D, h, g, :], pm[0:D, :], ACT.Gelu, bias=c_m1[:]).then_inc(s_mt, 1)
                            after(act, s_pg, 2 * b + 1 + g)
                            A.activation(gT[0:D, h, g, :], pg[0:D, :], ACT.Gelu, bias=c_g1[:]).then_inc(s_gt, 1)
                        return run

                    def tanh(g):
                        def run(b, n, h):
                            after(act, s_po, 2 * b + 1 + g)
                            after(act, s_pu, 2 * b - 6)
                            A.activation(gate[:, h, 4 * g:4 * g + 4, :], po[g][:, :, D:D + 1], ACT.Tanh,
                                         scale=0.5).then_inc(s_th, 1)
                        return run
                    skewed(act, (-2, slots), (3, gelus(0)), (4, tanh(0)), (3, gelus(1)), (4, tanh(1)), (2, keep),
                           (2, turned), (2, masks))

                @block.vector
                def _(dve):
                    own1, own = Own(dve, s_own1, 2), Own(dve, s_own, 2 * J - 1)
                    own.add(V.memset(S[:], 0.0))
                    own.do(V.memset(F[:], 0.0))
                    own.loop()

                    def step(b, n, h):
                        own1.step(b)
                        for g in range(2):
                            c = slice(4 * g, 4 * g + 4)
                            after(dve, s_th, 2 * b + 1 + g)
                            own1.do(V.tensor_scalar(gate[:, h, c, :], gate[:, h, c, :], 0.5, 0.5, ALU.mult, ALU.add))
                            V.tensor_tensor(g_[:, h, c, :], po[g][:, :, 0:D], gate[:, h, c, :].to_broadcast([P, 4, D]),
                                            ALU.mult).then_inc(s_pu, 1)
                        own1.end()
                        after(dve, s_pu, 2 * b + 2)
                        own.step(b)
                        after(dve, s_ms, b + 1)
                        dve.wait_ge(s_st[h], 16 * n)
                        scan_step(dve, own, h, D, g_[:, h], S, K, s_s, b + 1)
                        own.end()
                    skewed(dve, (4, step))
                    dve.wait_ge(s_cr, 1)
                    V.tensor_tensor(Z[:, 0:D], F[:, 0:D], pc[:], ALU.add).then_inc(s_z, 1)
        s_g.close(OF)
        retire()

        with ExitStack() as p4:
            ag = sb("n2_ag", [P, K, J, D], F32, p4)
            rec = sb("n2_rec", [P, K, J, TR], F32, p4)
            x1 = sb("n2_x1", [P, K, J, D], F32, p4)
            rT = sb("n2_rT", [D, 2, 2, 4 * P], F32, p4)
            aT = sb("n2_aT", [D, 2, 2, 4 * P], F32, p4)
            uT = sb("n2_uT", [D + 1, 2, 2, 4 * P], F32, p4)
            hs = sb("n2_h", [P, K, J, D], F32, p4)
            ln = sb("n2_ln", [P, K, J, D], F32, p4)
            x2 = sb("n2_x2", [P, K, J, D], F32, p4)
            y0 = sb("n2_y0", [P, K, J, D], F32, p4)
            st = sb("n2_st", [P, 2, J, 6], F32, p4)
            mv = sb("n2_mv", [P, K, J, 2], F32, p4)
            rn = sb("n2_rn", [P, K, 3, J], F32, p4)
            mv2 = sb("n2_mv2", [P, K, J, 2], F32, p4)
            rn2 = sb("n2_rn2", [P, K, 3, J], F32, p4)
            tr = [ps(f"n2_tr{g}", [P, 4 * P], p4) for g in range(2)]
            ta = [ps(f"n2_ta{g}", [P, 4 * P], p4) for g in range(2)]
            pu = [ps(f"n2_pu{g}", [P, 4 * P], p4) for g in range(2)]
            po = [ps(f"n2_po{g}", [P, 4, D], p4) for g in range(2)]
            s_r, s_x, s_g, s_st = quad("n2_rec_in"), quad("n2_x1_in"), s_stream[0], quad("n2_stored")
            s_ix, s_tr, s_ta, s_trc, s_tac, s_pu, s_ut, s_po, s_hs = map(sem, (
                "n2_rows_set", "n2_tr_full", "n2_ta_full", "n2_tr_copied", "n2_ta_copied", "n2_pu_full", "n2_gelu",
                "n2_po_full", "n2_h_ready"))
            s_mv, s_sd, s_rn, s_ln, s_x2, s_mv2, s_sd2, s_rn2, s_sn, s_y0 = map(sem, (
                "n2_stats", "n2_root", "n2_scale", "n2_ln_ready", "n2_x2_ready", "n2_stats2", "n2_root2", "n2_scale2",
                "n2_scale2_by_degree", "n2_y0_ready"))
            s_own1, s_own2, s_own3, s_own4, s_own5, s_one = map(sem, (
                "n2_vector_stats", "n2_vector_scale", "n2_vector_x2", "n2_vector_stats2", "n2_vector_scale2",
                "n2_ones"))
            with nc.Block() as block:
                @block.sync
                def _(sp):
                    def load(b, n, h):
                        after(sp, s_hs, 2 * b - 6)
                        sp.dma_start(rec[:, h], rows_of(rec_t, 0, b)).then_inc(s_r[h], 16)

                    def load_x1(b, n, h):
                        after(sp, s_x2, b - 3)
                        sp.dma_start(x1[:, h], rows_of(x1_t, 0, b)).then_inc(s_x[h], 16)

                    def store(b, n, h):
                        after(sp, s_x2, b + 1)
                        sp.dma_start(rows_of(x2_t, 0, b), x2[:, h]).then_inc(s_st[h], 16)
                        after(sp, s_y0, b + 1)
                        for t in y_t:
                            sp.dma_start(rows_of(t, 0, b), y0[:, h]).then_inc(s_st[h], 16)
                    skewed(sp, (0, load), (2, load_x1), (6, store))
                    for h in range(K):
                        sp.wait_ge(s_st[h], 48 * OF[h])

                @block.gpsimd
                def _(pool):
                    G.memset(uT[D:D + 1], 1.0).then_inc(s_one, 1)

                    def step(b, n, h):
                        after(pool, s_ix, b + 1)
                        after(pool, s_ta, 2 * b - 6)
                        gathers(agg1_t, lambda j: ag[:, h, j, :], h, s_g[h])
                    skewed(pool, (0, step))

                @block.tensor
                def _(pe):
                    pe.wait_ge(s_one, 1)

                    def turn(b, n, h):
                        pe.wait_ge(s_r[h], 16 * (n + 1))
                        s_g.wait(pe, h, 16 * J * (n + 1))
                        for g in range(2):
                            for bank, rows, full, used in ((tr, rec, s_tr, s_trc), (ta, ag, s_ta, s_tac)):
                                after(pe, used, 2 * b - 1 + g)
                                for j in range(4):
                                    last = T.transpose(bank[g][0:D, j * P:(j + 1) * P], rows[:, h, 4 * g + j, 0:D],
                                                       ident[:])
                                last.then_inc(full, 1)

                    def hidden(b, n, h):
                        for g in range(2):
                            after(pe, s_trc, 2 * b + 1 + g)
                            after(pe, s_tac, 2 * b + 1 + g)
                            after(pe, s_ut, 2 * b - 1 + g)
                            T.matmul(pu[g][0:D, :], w_ua[:], rT[:, h % 2, g, :], start=True, stop=False)
                            T.matmul(pu[g][0:D, :], w_ub[:], aT[:, h % 2, g, :], start=False, stop=True
                                     ).then_inc(s_pu, 1)

                    def outer_layer(b, n, h):
                        for g in range(2):
                            after(pe, s_ut, 2 * b + 1 + g)
                            after(pe, s_hs, 2 * b - 1 + g)
                            for j in range(4):
                                last = T.matmul(po[g][:, j, :], uT[:, h % 2, g, j * P:(j + 1) * P], w_u2[:],
                                                start=True, stop=True)
                            last.then_inc(s_po, 1)
                    skewed(pe, (3, outer_layer), (2, hidden), (1, turn))

                @block.scalar
                def _(act):
                    def slots(b, n, h):
                        s_g.wait(act, h, 16 * J * n)
                        A.copy(idx_s[:, h, :], cols(ptr_i, b)).then_inc(s_ix, 1)

                    def gelu(b, n, h):
                        after(act, s_po, 2 * b - 2)
                        for g in range(2):
                            after(act, s_pu, 2 * b + 1 + g)
                            A.activation(uT[0:D, h % 2, g, :], pu[g][0:D, :], ACT.Gelu, bias=c_u1[:]
                                         ).then_inc(s_ut, 1)

                    def norm(b, n, h):
                        after(act, s_x2, b - 3)
                        ln_norm(act, b, hs[:, h], ln[:, h], rn[:, h], s_rn, ACT.Identity).then_inc(s_ln, 1)

                    def norm2(b, n, h):
                        act.wait_ge(s_st[h], 48 * n)
                        ln_norm(act, b, x2[:, h], y0[:, h], rn2[:, h], s_sn, ACT.Relu).then_inc(s_y0, 1)
                    skewed(act, (-2, slots), (4, norm), (6, norm2), (2, gelu),
                           (3, lambda b, n, h: ln_root(act, b, mv[:, h], rn[:, h], s_mv, s_sd)),
                           (5, lambda b, n, h: ln_root(act, b, mv2[:, h], rn2[:, h], s_mv2, s_sd2)))

                @block.vector
                def _(dve):
                    own1, own2, own3, own4, own5 = (Own(dve, s_own1, 1), Own(dve, s_own2, 1), Own(dve, s_own3, 1),
                                                    Own(dve, s_own4, 1), Own(dve, s_own5, 2))

                    def turned(b, n, h):
                        after(dve, s_pu, 2 * b - 2)
                        for g in range(2):
                            after(dve, s_tr, 2 * b + 1 + g)
                            V.tensor_copy(rT[:, h % 2, g, :], tr[g][0:D, :]).then_inc(s_trc, 1)
                            after(dve, s_ta, 2 * b + 1 + g)
                            V.tensor_copy(aT[:, h % 2, g, :], ta[g][0:D, :]).then_inc(s_tac, 1)

                    def add(b, n, h):
                        after(dve, s_ln, b - 3)
                        for g in range(2):
                            c = slice(4 * g, 4 * g + 4)
                            after(dve, s_po, 2 * b + 1 + g)
                            V.tensor_tensor(hs[:, h, c, :], rec[:, h, c, 0:D], po[g][:], ALU.add).then_inc(s_hs, 1)
                        after(dve, s_hs, 2 * b + 2)
                        after(dve, s_rn, b - 3)
                        ln_stats(dve, own1, b, hs[:, h], st[:, 0], mv[:, h], s_mv)

                    def scale(b, n, h):
                        after(dve, s_ln, b - 3)
                        own2.step(b)
                        ln_scale(dve, own2, b, mv[:, h], rn[:, h], s_sd, s_rn)

                    def update(b, n, h):
                        own3.step(b)
                        after(dve, s_ln, b + 1)
                        own3.do(V.tensor_tensor(ln[:, h], ln[:, h], r_all[:, 0:1, :].to_broadcast([P, J, D]), ALU.mult))
                        own3.end()
                        dve.wait_ge(s_x[h], 16 * (n + 1))
                        dve.wait_ge(s_st[h], 48 * n)
                        V.tensor_tensor(x2[:, h], x1[:, h], ln[:, h], ALU.add).then_inc(s_x2, 1)
                        after(dve, s_x2, b + 1)
                        after(dve, s_sn, b - 3)
                        ln_stats(dve, own4, b, x2[:, h], st[:, 1], mv2[:, h], s_mv2)

                    def scale2(b, n, h):
                        after(dve, s_y0, b - 3)
                        own5.step(b)
                        ln_scale(dve, own5, b, mv2[:, h], rn2[:, h], s_sd2, s_rn2)
                        after(dve, s_rn2, b + 1)
                        own5.add(V.tensor_tensor(rn2[:, h, 0, :], rn2[:, h, 0, :], cols(iroot, b), ALU.mult))
                        own5.end()
                        V.tensor_tensor(rn2[:, h, 1, :], rn2[:, h, 1, :], cols(iroot, b), ALU.mult).then_inc(s_sn, 1)
                    skewed(dve, (4, scale), (6, scale2), (3, add), (5, update), (1, turned))
        s_g.close(OF)
        retire()

        with ExitStack() as p5:
            H = sb("H", [P, CH, D], F32, p5)
            g_ = sb("r_g", [P, GB, J, D], F32, p5)
            cs = sb("r_c", [P, 2, J, D], F32, p5)
            S = sb("r_S", [P, 2, J, D], F32, p5)
            z0 = sb("r_z0", [P, D], F32, p5)
            zs = sb("r_zs", [P, D], F32, p5)
            zc = sb("r_zc", [P, D], F32, p5)
            idx_z = sb("idx_z", [P, 1], I32, p5)
            t_ = sb("r_t", [P, CH], F32, p5)
            yptr_e = sb("yptr_e", [P, CH], I32, p5)
            dst_s = sb("r_dst_s", [P, 2, J], I32, p5)
            pc = ps("r_pc", [P, D], p5)
            k_wide = lambda n, h: cols(k_e, 2 * n + h).unsqueeze(2).to_broadcast([P, J, D])

            def finish_round(dve, own, s_cr, count, before, s_z):
                dve.wait_ge(s_cr, count)
                own.do(V.tensor_tensor(Z[:, 0:D], F[:, 0:D], pc[:], ALU.add))
                own.add(V.memset(F[:], 0.0))
                own.do(V.tensor_tensor(Z[:, 0:D], Z[:, 0:D], before[:], ALU.add))
                V.scalar_tensor_tensor(out=zs[:], in0=Z[:, 0:D], scalar=k_z[:], in1=z0[:], op0=ALU.mult,
                                       op1=ALU.add).then_inc(s_z, 1)

            s_v, s_ix, s_g, s_c, s_s, s_st, s_ct = (
                sem("r1_vector"), sems("r1_rows_set"), s_stream[0], s_stream[1], sems("r1_values"), sems("r1_stored"), sems("r1_start_stored"))
            s_cr, s_z, s_zo, s_c0, s_i0 = (sem("r1_carry"), sem("r1_first_values"), sem("r1_first_stored"),
                                           s_single, sem("r1_first_rows"))
            s_cw = sems("r1_start_term")
            with nc.Block() as block:
                @block.sync
                def _(sp):
                    def step(n, h):
                        sp.wait_ge(s_cw[h], n + 1)
                        sp.dma_start(rows_of(c_t, 0, 2 * n + h), cs[:, h]).then_inc(s_ct[h], 16)
                        sp.wait_ge(s_s[h], n + 1)
                        sp.sem_inc(s_turn_s)
                        sp.dma_start(rows_of(y_t[0], VALUES, 2 * n + h), cols(H, 2 * n + h)).then_inc(s_st[h], 16)
                    batches(sp, step)
                    sp.wait_ge(s_z, 1)
                    sp.dma_start(y_t[0][VALUES + AUX:VALUES + AUX + P, :], zs[:]).then_inc(s_zo, 16)
                    for s in (s_ct, s_st):
                        sp.wait_ge(s[0], 16 * (PAIRS + 1))
                        sp.wait_ge(s[1], 16 * PAIRS)
                    sp.wait_ge(s_zo, 16)

                @block.gpsimd
                def _(pool):
                    pool.wait_ge(s_i0, 1)
                    G.indirect_dma_start(out=zc[:], out_offset=None, in_=y_t[0][0:ROWS, :],
                                         in_offset=bass.IndirectOffsetOnAxis(ap=idx_z[:], axis=0)).then_inc(s_c0, 16)

                    def step(n, h):
                        pool.wait_ge(s_ix[h], 3 * n + 3)
                        pool.wait_ge(s_s[h], n)
                        pool.wait_ge(s_ct[h], 16 * n)
                        gathers(y_t[0][0:ROWS, :], lambda j: g_[:, h, j, :], h, s_g[h])
                        for j in range(J):
                            G.indirect_dma_start(out=cs[:, h, j, :], out_offset=None, in_=y_t[0][0:ROWS, :],
                                                 in_offset=bass.IndirectOffsetOnAxis(ap=dst_s[:, h, j:j + 1], axis=0)
                                                 ).then_inc(s_c[h], 16)
                    batches(pool, step)

                @block.tensor
                def _(pe):
                    pe.wait_ge(s_s[0], PAIRS + 1)
                    T.matmul(pc[:], B[:], S[:, 0, J - 1, :], start=True, stop=True).then_inc(s_cr, 1)

                @block.scalar
                def _(act):
                    A.copy(idx_z[:], dst_i[:, 0:1]).then_inc(s_i0, 1)

                    def step(n, h):
                        s_g.wait(act, h, 16 * J * n)
                        s_c.wait(act, h, 16 * J * n)
                        act.wait_ge(s_s[h], n)
                        A.copy(idx_s[:, h, :], cols(src_i, 2 * n + h)).then_inc(s_ix[h], 1)
                        A.copy(dst_s[:, h, :], cols(dst_i, 2 * n + h)).then_inc(s_ix[h], 1)
                        A.copy(scan_s[:, h], cols(scan, 2 * n + h)).then_inc(s_ix[h], 1)
                    batches(act, step)

                @block.vector
                def _(dve):
                    own = Own(dve, s_v, 2 * J + 2)
                    own.add(V.memset(S[:], 0.0))
                    own.do(V.memset(F[:], 0.0))
                    t = H[:, 0:5, :].rearrange("p a d -> p (a d)")[:, 0:CH]
                    no = H[:, 5:10, :].rearrange("p a d -> p (a d)")[:, 0:CH]
                    own.add(V.tensor_scalar(no, ptr_e[:], float(ZROW), None, ALU.is_equal))
                    own.do(V.tensor_copy(t, src_i[:]))
                    pointers(own, ptr_e, no, t, t_[:], yptr_e, VALUES)
                    own.settle()
                    dve.wait_ge(s_c0, 16)
                    own.do(V.tensor_scalar(z0[:], zc[:], ALPHA, None, ALU.mult))
                    own.do(V.reciprocal(t_[:], k_e[:]))
                    own.do(V.tensor_scalar(t_[:], t_[:], ALPHA, None, ALU.mult))
                    own.loop()

                    def step(n, h):
                        own.step(2 * n + h)
                        s_g.wait(dve, h, 16 * J * (n + 1))
                        scan_step(dve, own, h, D, g_[:, h], S)
                        s_c.wait(dve, h, 16 * J * (n + 1))
                        v = cols(H, 2 * n + h)
                        own.do(V.tensor_tensor(v, S[:, h], cs[:, h], ALU.add))
                        V.tensor_tensor(cs[:, h], cs[:, h], cols(t_, 2 * n + h).unsqueeze(2).to_broadcast([P, J, D]),
                                        ALU.mult).then_inc(s_cw[h], 1)
                        dve.wait_ge(s_cw[h], n + 1)
                        own.do(V.tensor_tensor(v, v, cs[:, h], ALU.add))
                        V.tensor_tensor(v, v, k_wide(n, h), ALU.mult).then_inc(s_s[h], 1)
                        own.end()

                    batches(dve, step)
                    finish_round(dve, own, s_cr, 1, zc, s_z)
            s_g.close(PER)
            s_c.close(PER)
            retire()

            pu = [[ps(f"r_pu{h}{g}", [P, 4, D], p5) for g in range(2)] for h in range(2)]
            s_v, s_ix, s_g, s_up, s_s, s_st, s_ss = (sem("r_vector"), sem("r_rows_set"), s_stream[2],
                                                     sem("r_summed"), sem("r_values"), sem("r_stored"), sem("r_sums"))
            s_c = sems("r_start_loaded")
            s_cr, s_z, s_zo = sem("r_carry"), sem("r_first_values"), sem("r_first_stored")

            def rounds(eng, one):
                one(0, 0)
                with eng.Fori(0, ROUNDS // 2 - 1) as q:
                    one(2 * q + 1, 1)
                    one(2 * q + 2, 0)

            with nc.Block() as block:
                @block.sync
                def _(sp):
                    def one(r, odd):
                        to = y_t[1 - odd]

                        def load(b, n, h):
                            after(sp, s_up, r * NB + b - 1)
                            sp.sem_inc(s_turn_s)
                            sp.dma_start(cs[:, h % 2], rows_of(c_t, 0, b)).then_inc(s_c[h % 2], 16)

                        def store(b, n, h):
                            after(sp, s_s, r * NB + b + 1)
                            sp.sem_inc(s_turn_s)
                            sp.dma_start(rows_of(to, VALUES, b), cols(H, b)).then_inc(s_st, 16)
                        after(sp, s_up, r * NB)
                        sp.sem_inc(s_turn_s)
                        skewed(sp, (1, store), (-1, load))
                        after(sp, s_z, r + 1)
                        sp.dma_start(to[VALUES + AUX:VALUES + AUX + P, :], zs[:]).then_inc(s_zo, 16)
                    rounds(sp, one)
                    sp.wait_ge(s_st, 16 * (ROUNDS - 1) * NB)
                    sp.wait_ge(s_zo, 16 * (ROUNDS - 1))

                @block.gpsimd
                def _(pool):
                    def one(r, odd):
                        after(pool, s_st, 16 * NB * r)
                        after(pool, s_zo, 16 * r)
                        pool.sem_inc(s_turn_p)

                        def step(b, n, h):
                            after(pool, s_ix, 2 * (r * NB + b) + 2)
                            after(pool, s_ss, r * NB + b + 1 - GB)
                            gathers(y_t[odd], lambda j: g_[:, h % GB, j, :], h, s_g[h])
                        skewed(pool, (0, step))
                    rounds(pool, one)

                @block.tensor
                def _(pe):
                    def one(r, odd):
                        def start(b, n, h):
                            pe.wait_ge(s_c[h % 2], 16 * (r * PER[h % 2] + 2 * n + h // 2 + 1))
                            after(pe, s_s, r * NB + b - 1)
                            for g in range(2):
                                c = slice(4 * g, 4 * g + 4)
                                T.matmul(pu[h % 2][g][:], ident[:], cols(H, b)[:, c, :], start=True, stop=False)
                                T.matmul(pu[h % 2][g][:], ident[:], cs[:, h % 2, c, :], start=False, stop=False)

                        def add(b, n, h):
                            after(pe, s_ss, r * NB + b + 1)
                            for g in range(2):
                                last = T.matmul(pu[h % 2][g][:], ident[:], S[:, h % 2, 4 * g:4 * g + 4, :],
                                                start=False, stop=True)
                            last.then_inc(s_up, 1)
                        after(pe, s_s, r * NB)
                        skewed(pe, (0, add), (-1, start))
                        T.matmul(pc[:], B[:], S[:, 0, J - 1, :], start=True, stop=True).then_inc(s_cr, 1)
                    rounds(pe, one)

                @block.scalar
                def _(act):
                    def one(r, odd):
                        def slots(b, n, h):
                            s_g.wait(act, h, 16 * J * (r * OF[h] + n))
                            A.copy(idx_s[:, h, :], cols(yptr_e, b)).then_inc(s_ix, 1)
                            after(act, s_ss, r * NB + b - 3)
                            A.copy(scan_s[:, h], cols(scan, b)).then_inc(s_ix, 1)

                        def value(b, n, h):
                            after(act, s_up, r * NB + b + 1)
                            v, k = cols(H, b), cols(k_e, b)
                            for j in range(J):
                                last = A.activation(v[:, j, :], pu[h % 2][j // 4][:, j % 4, :], ACT.Copy,
                                                    scale=k[:, j:j + 1])
                            last.then_inc(s_s, 1)
                        after(act, s_ss, r * NB)
                        skewed(act, (-2, slots), (1, value))
                    rounds(act, one)

                @block.vector
                def _(dve):
                    own = Own(dve, s_v)
                    per_batch = 2 * J - 1
                    per_round = NB * per_batch + 3

                    def one(r, odd):
                        def step(b, n, h):
                            own.base, own.n = r * per_round + b * per_batch, 0
                            after(dve, s_ix, 2 * (r * NB + b) + 2)
                            after(dve, s_up, r * NB + b - 1)
                            s_g.wait(dve, h, 16 * J * (r * OF[h] + n + 1))
                            scan_step(dve, own, h, D, g_[:, h % GB], S, 2, s_ss, r * NB + b + 1)
                            assert own.n == per_batch
                            dve.sem_inc(s_turn_v)
                        skewed(dve, (0, step))
                        own.base, own.n = r * per_round + NB * per_batch, 0
                        finish_round(dve, own, s_cr, r + 1, zs, s_z)
                        assert own.n == 3
                        dve.wait_ge(s_z, r + 1)
                        dve.sem_inc(s_turn_v)
                    rounds(dve, one)
        s_g.close(OF, ROUNDS - 1)
        retire()

        with ExitStack() as p6:
            yg = sb("n3_y", [P, K, J, D], F32, p6)
            xs = sb("n3_x", [P, K, J, D], F32, p6)
            h3 = sb("n3_h", [P, K, J, D], F32, p6)
            hT = sb("n3_hT", [D, K, 2, 4 * P], F32, p6)
            zt = sb("n3_z", [P, K, J, D], F32, p6)
            st = sb("n3_st", [P, K, J, 6], F32, p6)
            mv = sb("n3_mv", [P, K, J, 2], F32, p6)
            rn = sb("n3_rn", [P, K, 3, J], F32, p6)
            tp = [ps(f"n3_tp{g}", [P, 4 * P], p6) for g in range(2)]
            po = [ps(f"n3_po{g}", [P, 4, D], p6) for g in range(2)]
            s_x, s_g, s_st, s_sz = quad("n3_x_in"), s_stream[0], quad("n3_x3_stored"), quad("n3_z_stored")
            s_ix, s_x3, s_mv, s_sd, s_rn, s_h, s_tp, s_tc, s_po, s_pu, s_own0, s_own1, s_own2 = map(sem, (
                "n3_rows_set", "n3_x_updated", "n3_stats", "n3_root", "n3_scale", "n3_h_ready", "n3_tp_full",
                "n3_tp_copied", "n3_po_full", "n3_po_used", "n3_vector_x", "n3_vector_stats", "n3_vector_scale"))
            with nc.Block() as block:
                @block.sync
                def _(sp):
                    def load(b, n, h):
                        sp.wait_ge(s_st[h], 16 * n)
                        sp.sem_inc(s_turn_s)
                        after(sp, s_h, b - 3)
                        sp.sem_inc(s_turn_s)
                        sp.dma_start(xs[:, h], rows_of(x2_t, 0, b)).then_inc(s_x[h], 16)

                    def store(b, n, h):
                        after(sp, s_x3, b + 1)
                        sp.dma_start(rows_of(x3_t, 0, b), xs[:, h]).then_inc(s_st[h], 16)

                    def store_z(b, n, h):
                        after(sp, s_pu, 2 * b + 2)
                        sp.dma_start(rows_of(z_t, 0, b), zt[:, h]).then_inc(s_sz[h], 16)
                    skewed(sp, (0, load), (1, store), (4, store_z))
                    for h in range(K):
                        sp.wait_ge(s_st[h], 16 * OF[h])
                        sp.wait_ge(s_sz[h], 16 * OF[h])

                @block.gpsimd
                def _(pool):
                    def step(b, n, h):
                        after(pool, s_ix, b + 1)
                        after(pool, s_x3, b - 3)
                        gathers(y_t[1], lambda j: yg[:, h, j, :], h, s_g[h])
                    skewed(pool, (0, step))

                @block.vector
                def _(dve):
                    own0, own1, own2 = Own(dve, s_own0, 1), Own(dve, s_own1, 1), Own(dve, s_own2, 1)

                    def add(b, n, h):
                        own0.step(b)
                        s_g.wait(dve, h, 16 * J * (n + 1))
                        own0.do(V.tensor_tensor(yg[:, h], yg[:, h], cols(root, b).unsqueeze(2).to_broadcast([P, J, D]),
                                                ALU.mult))
                        own0.end()
                        dve.wait_ge(s_x[h], 16 * (n + 1))
                        V.tensor_tensor(xs[:, h], xs[:, h], yg[:, h], ALU.add).then_inc(s_x3, 1)
                        after(dve, s_x3, b + 1)
                        after(dve, s_rn, b - 3)
                        ln_stats(dve, own1, b, xs[:, h], st[:, h], mv[:, h], s_mv)

                    def scale(b, n, h):
                        after(dve, s_h, b - 3)
                        own2.step(b)
                        ln_scale(dve, own2, b, mv[:, h], rn[:, h], s_sd, s_rn)

                    def weigh(b, n, h):
                        dve.wait_ge(s_sz[h], 16 * n)
                        for g in range(2):
                            c = slice(4 * g, 4 * g + 4)
                            after(dve, s_po, 2 * b + 1 + g)
                            V.tensor_tensor(zt[:, h, c, :], po[g][:],
                                            cols(dinv, b)[:, c].unsqueeze(2).to_broadcast([P, 4, D]),
                                            ALU.mult).then_inc(s_pu, 1)
                    skewed(dve, (2, scale), (4, weigh), (1, add))

                @block.scalar
                def _(act):
                    def slots(b, n, h):
                        s_g.wait(act, h, 16 * J * n)
                        A.copy(idx_s[:, h, :], cols(yptr_i, b)).then_inc(s_ix, 1)

                    def norm(b, n, h):
                        after(act, s_tp, 2 * b - 6)
                        ln_norm(act, b, xs[:, h], h3[:, h], rn[:, h], s_rn, ACT.Relu).then_inc(s_h, 1)

                    def turned(b, n, h):
                        after(act, s_po, 2 * b - 6)
                        for g in range(2):
                            after(act, s_tp, 2 * b + 1 + g)
                            A.copy(hT[:, h, g, :], tp[g][0:D, :]).then_inc(s_tc, 1)
                    skewed(act, (-2, slots), (2, norm), (3, turned),
                           (1, lambda b, n, h: ln_root(act, b, mv[:, h], rn[:, h], s_mv, s_sd)))

                @block.tensor
                def _(pe):
                    def turn(b, n, h):
                        after(pe, s_h, b + 1)
                        for g in range(2):
                            after(pe, s_tc, 2 * b + g - 1)
                            for j in range(4):
                                last = T.transpose(tp[g][0:D, j * P:(j + 1) * P], h3[:, h, 4 * g + j, :], ident[:])
                            last.then_inc(s_tp, 1)

                    def product(b, n, h):
                        for g in range(2):
                            after(pe, s_tc, 2 * b + 1 + g)
                            after(pe, s_pu, 2 * b - 1 + g)
                            for j in range(4):
                                last = T.matmul(po[g][:, j, :], hT[:, h, g, j * P:(j + 1) * P], w_3[:],
                                                start=True, stop=True)
                            last.then_inc(s_po, 1)
                    skewed(pe, (4, product), (3, turn))
        s_g.close(OF)
        retire()

        with ExitStack() as p7:
            g_ = sb("e3_g", [P, 2, J, D], F32, p7)
            S = sb("e3_S", [P, 2, J, D], F32, p7)
            pc = ps("e3_pc", [P, D], p7)
            s_ix, s_g, s_s, s_st = sems("e3_rows_set"), s_stream[0], sems("e3_sums"), sems("e3_stored")
            s_own, s_cr, s_z, s_zo = sem("e3_vector"), sem("e3_carry"), sem("e3_first_sums"), sem("e3_first_stored")
            with nc.Block() as block:
                @block.sync
                def _(sp):
                    def step(n, h):
                        sp.wait_ge(s_s[h], n + 1)
                        sp.dma_start(rows_of(agg3_t, 0, 2 * n + h), S[:, h]).then_inc(s_st[h], 16)
                    batches(sp, step)
                    sp.wait_ge(s_z, 1)
                    sp.dma_start(agg3_t[AUX:AUX + P, :], Z[:, 0:D]).then_inc(s_zo, 16)
                    sp.wait_ge(s_st[0], 16 * (PAIRS + 1))
                    sp.wait_ge(s_st[1], 16 * PAIRS)
                    sp.wait_ge(s_zo, 16)

                @block.gpsimd
                def _(pool):
                    def step(n, h):
                        pool.wait_ge(s_ix[h], 2 * n + 2)
                        pool.wait_ge(s_s[h], n)
                        gathers(z_t, lambda j: g_[:, h, j, :], h, s_g[h])
                    batches(pool, step)

                @block.tensor
                def _(pe):
                    pe.wait_ge(s_s[0], PAIRS + 1)
                    T.matmul(pc[:], B[:], S[:, 0, J - 1, :], start=True, stop=True).then_inc(s_cr, 1)

                @block.scalar
                def _(act):
                    def step(n, h):
                        act.wait_ge(s_s[h], n)
                        gather_slots(act, n, h, src_i, s_ix, s_g, 16 * J)
                        A.copy(scan_s[:, h], cols(scan, 2 * n + h)).then_inc(s_ix[h], 1)
                    batches(act, step)

                @block.vector
                def _(dve):
                    own = Own(dve, s_own, 1 + 2 * J - 1)
                    own.add(V.memset(S[:], 0.0))
                    own.do(V.memset(F[:], 0.0))
                    own.loop()

                    def step(n, h):
                        own.step(2 * n + h)
                        dve.wait_ge(s_ix[h], 2 * n + 2)
                        s_g.wait(dve, h, 16 * J * (n + 1))
                        own.do(V.tensor_tensor(g_[:, h], g_[:, h], scan_s[:, h, :, 2:3].to_broadcast([P, J, D]),
                                               ALU.mult))
                        dve.wait_ge(s_st[h], 16 * n)
                        scan_step(dve, own, h, D, g_[:, h], S, 2, s_s[h], n + 1)
                        own.end()
                    batches(dve, step)
                    dve.wait_ge(s_cr, 1)
                    V.tensor_tensor(Z[:, 0:D], F[:, 0:D], pc[:], ALU.add).then_inc(s_z, 1)
        s_g.close(PER)
        retire()

        with ExitStack() as p8:
            ag = sb("n4_ag", [P, 2, J, D], F32, p8)
            zt = sb("n4_z", [P, 2, J, D], F32, p8)
            xs = sb("n4_x", [P, 2, J, D], F32, p8)
            o_ = sb("n4_o", [P, 2, J, D], F32, p8)
            s_x, s_ix, s_g, s_o, s_st = (sems("n4_in"), sems("n4_rows_set"), s_stream[0], sems("n4_out"),
                                         sems("n4_stored"))
            s_own, s_t = sem("n4_vector"), sem("n4_tail_stored")
            out_v = out[0:FULL * CH, :].rearrange("(p j) d -> p j d", j=CH)
            with nc.Block() as block:
                @block.sync
                def _(sp):
                    def load(n, h):
                        sp.wait_ge(s_o[h], n)
                        sp.dma_start(zt[:, h], rows_of(z_t, 0, 2 * n + h)).then_inc(s_x[h], 16)
                        sp.dma_start(xs[:, h], rows_of(x3_t, 0, 2 * n + h)).then_inc(s_x[h], 16)

                    def store(n, h):
                        sp.wait_ge(s_o[h], n + 1)
                        c = bass.ds((2 * n + h) * J, J)
                        sp.dma_start(out_v[0:SPLIT, c, :], o_[0:SPLIT, h]).then_inc(s_st[h], 16)
                        sp.dma_start(out_v[SPLIT:FULL, c, :], o_[SPLIT:FULL, h]).then_inc(s_st[h], 16)
                        sp.dma_start(out_tail.rearrange("(a j) d -> a j d", a=1)[:, c, :], o_[FULL:P, h]
                                     ).then_inc(s_st[h], 16)
                    ahead(sp, load, store)
                    sp.wait_ge(s_st[0], 48 * (PAIRS + 1))
                    sp.wait_ge(s_st[1], 48 * PAIRS)
                    sp.dma_start(out[FULL * CH:N, :], out_tail[0:TAIL, :]).then_inc(s_t, 16)
                    sp.wait_ge(s_t, 16)

                @block.gpsimd
                def _(pool):
                    def step(n, h):
                        pool.wait_ge(s_ix[h], n + 1)
                        pool.wait_ge(s_o[h], n)
                        gathers(agg3_t, lambda j: ag[:, h, j, :], h, s_g[h])
                    batches(pool, step)

                @block.scalar
                def _(act):
                    def step(n, h):
                        gather_slots(act, n, h, ptr_i, s_ix, s_g, 16 * J)
                    batches(act, step)

                @block.vector
                def _(dve):
                    own = Own(dve, s_own, 3)

                    def step(n, h):
                        own.step(2 * n + h)
                        dve.wait_ge(s_x[h], 32 * (n + 1))
                        own.add(V.tensor_tensor(xs[:, h], xs[:, h], r_all[:, 2:3, :].to_broadcast([P, J, D]), ALU.add))
                        s_g.wait(dve, h, 16 * J * (n + 1))
                        own.do(V.tensor_tensor(ag[:, h], ag[:, h], zt[:, h], ALU.add))
                        own.do(V.tensor_tensor(ag[:, h], ag[:, h], cols(dinv, 2 * n + h).unsqueeze(2).to_broadcast([P, J, D]),
                                               ALU.mult))
                        dve.wait_ge(s_st[h], 48 * n)
                        V.tensor_tensor(o_[:, h], ag[:, h], xs[:, h], ALU.add).then_inc(s_o[h], 1)
                        own.end()
                    batches(dve, step)


_INS = ['x', 'src', 'dst', 'edge_attr_32', 'edge_attr_96', 'edge_weight',
        'L0_gnn_Wq', 'L0_gnn_bq', 'L0_gnn_Wk', 'L0_gnn_bk', 'L0_gnn_We', 'L0_gnn_be', 'L0_gnn_Wv', 'L0_gnn_bv',
        'L1_gnn_mW1', 'L1_gnn_mb1', 'L1_gnn_mW2', 'L1_gnn_mb2', 'L1_gnn_gW1', 'L1_gnn_gb1', 'L1_gnn_gW2',
        'L1_gnn_gb2', 'L1_gnn_uW1', 'L1_gnn_ub1', 'L1_gnn_uW2', 'L1_gnn_ub2', 'L1_gnn_ln_g', 'L1_gnn_ln_b',
        'L3_gnn_W', 'L3_gnn_b']


def kernel(**inputs):
    import numpy as _np
    import concourse.bacc as _bacc
    from concourse import mybir as _mybir
    from concourse.bass_utils import run_bass_kernel_spmd as _run

    nc = _bacc.Bacc("TRN2", target_bir_lowering=False, num_devices=1)
    arrays, args = {}, []
    for name in _INS:
        a = _np.ascontiguousarray(inputs[name])
        arrays[f"in_{name}"] = a
        args.append(nc.dram_tensor(f"in_{name}", a.shape, _mybir.dt.from_np(a.dtype), kind="ExternalInput").ap())
    args.append(nc.dram_tensor("out_0", (N, D), F32, kind="ExternalOutput").ap())
    program(nc, *args)
    r = _run(nc, [arrays], core_ids=[0])
    return r.results[0]["out_0"]
```
